# Optimizing a Trainium2 kernel written in Bass

```python
import numpy as np
import jax
import jax.numpy as jnp

def _softmax(x, axis=-1):
    return jax.nn.softmax(x, axis=axis)

def _gelu(x):
    return jax.nn.gelu(x, approximate=True)

def _silu(x):
    return jax.nn.silu(x)

def _sigmoid(x):
    return jax.nn.sigmoid(x)

def _layernorm(x, axis=-1, eps=1e-05):
    m = jnp.mean(x, axis=axis, keepdims=True)
    v = jnp.var(x, axis=axis, keepdims=True)
    return (x - m) / jnp.sqrt(v + eps)

def _scatter_add(tgt, idx, src, axis=0):
    return tgt.at[idx].add(src)

def _segment_sum(src, seg, n):
    return jax.ops.segment_sum(src, seg, n)
kernel_name = 'mk_gnn_resnorm_d2_gnn_r32_732ed7'

def setup_inputs(seed: int=0):
    np.random.seed(seed)
    _w = jnp.asarray

    def _rec_inputs():
        import jax
        import jax.numpy as jnp
        _gk = jax.random.key(seed)
        x = -0.000202 + 1 * jax.random.normal(jax.random.fold_in(_gk, 1), (50000, 128), jnp.float32)
        src = jax.random.randint(jax.random.fold_in(_gk, 2), (25000,), 0, 50000, jnp.int32)
        dst = jax.random.randint(jax.random.fold_in(_gk, 3), (25000,), 0, 50000, jnp.int32)
        _o = jnp.argsort(dst, stable=True)
        src = src[_o]
        dst = dst[_o]
        edge_attr_128 = 5.93493e-05 + 1.00006 * jax.random.normal(jax.random.fold_in(_gk, 12), (25000, 128), jnp.float32)
        edge_weight1 = jax.random.uniform(jax.random.fold_in(_gk, 14), (25000, 1), jnp.float32, 0.0, 0.999998)
        return (x, src, dst, edge_attr_128, edge_weight1)
    x, src, dst, edge_attr_128, edge_weight1 = _rec_inputs()

    def _L0_gnn_setup():
        import jax, jax.numpy as jnp
        import numpy as np
        N, E, D = (50000, 18750, 128)

        def spline_conv(x, src, dst, u, W, root, bias):
            n = x.shape[0]
            h = jnp.einsum('nd,kdo->kno', x, W)
            msg = (1.0 - u)[:, None] * h[0][src] + u[:, None] * h[1][src]
            agg = jax.ops.segment_sum(msg, dst, num_segments=n)
            cnt = jax.ops.segment_sum(jnp.ones_like(u), dst, num_segments=n)
            agg = agg / jnp.maximum(cnt, 1.0)[:, None]
            return agg + x @ root + bias
        key = jax.random.key(seed)
        ks = jax.random.split(key, 9)
        s = 1.0 / np.sqrt(D).astype(np.float32)
        return {'x': jax.random.normal(ks[0], (N, D), dtype=jnp.float32), 'edge_index': jax.random.randint(ks[1], (2, E), 0, N, dtype=jnp.int32), 'pseudo': jax.random.uniform(ks[2], (E, 1), dtype=jnp.float32), 'W1': jax.random.normal(ks[3], (2, D, D), dtype=jnp.float32) * s, 'root1': jax.random.normal(ks[4], (D, D), dtype=jnp.float32) * s, 'b1': jnp.zeros((D,), dtype=jnp.float32), 'W2': jax.random.normal(ks[5], (2, D, D), dtype=jnp.float32) * s, 'root2': jax.random.normal(ks[6], (D, D), dtype=jnp.float32) * s, 'b2': jnp.zeros((D,), dtype=jnp.float32)}
    _L0_gnn_all = _L0_gnn_setup()
    _L0_gnn_in = {k: v for k, v in _L0_gnn_all.items() if k in ('W1', 'root1', 'b1', 'W2', 'root2', 'b2')}
    del _L0_gnn_all

    def _L1_gnn_setup():
        import jax, jax.numpy as jnp
        import numpy as np
        N_NODES = 50000
        N_EDGES = 18750
        D = 128
        N_GRAPHS = 64
        key = jax.random.key(seed)
        ks = jax.random.split(key, 10)
        inp = {'x': jax.random.normal(ks[0], (N_NODES, D), jnp.float32), 'edge_index': jax.random.randint(ks[1], (2, N_EDGES), 0, N_NODES, jnp.int64), 'edge_attr': jax.random.normal(ks[2], (N_EDGES, D), jnp.float32), 'u': jax.random.normal(ks[3], (N_GRAPHS, D), jnp.float32), 'batch': jnp.sort(jax.random.randint(ks[4], (N_NODES,), 0, N_GRAPHS, jnp.int64)), 'W1a': jax.random.normal(ks[5], (2 * D, 256), jnp.float32) * (1.0 / np.sqrt(2 * D)), 'b1a': jnp.zeros((256,), jnp.float32), 'W1b': jax.random.normal(ks[6], (256, D), jnp.float32) * (1.0 / 16.0), 'b1b': jnp.zeros((D,), jnp.float32), 'W2a': jax.random.normal(ks[7], (3 * D, 256), jnp.float32) * (1.0 / np.sqrt(3 * D)), 'b2a': jnp.zeros((256,), jnp.float32), 'W2b': jax.random.normal(ks[8], (256, D), jnp.float32) * (1.0 / 16.0), 'b2b': jnp.zeros((D,), jnp.float32)}
        return inp
    _L1_gnn_all = _L1_gnn_setup()
    _L1_gnn_in = {k: v for k, v in _L1_gnn_all.items() if k in ('u', 'W1a', 'b1a', 'W1b', 'b1b', 'W2a', 'b2a', 'W2b', 'b2b')}
    del _L1_gnn_all
    return {'x': x, 'src': src, 'dst': dst, 'edge_attr_128': edge_attr_128, 'edge_weight1': edge_weight1, 'L0_gnn_W1': _L0_gnn_in['W1'], 'L0_gnn_root1': _L0_gnn_in['root1'], 'L0_gnn_b1': _L0_gnn_in['b1'], 'L0_gnn_W2': _L0_gnn_in['W2'], 'L0_gnn_root2': _L0_gnn_in['root2'], 'L0_gnn_b2': _L0_gnn_in['b2'], 'L1_gnn_u': _L1_gnn_in['u'], 'L1_gnn_W1a': _L1_gnn_in['W1a'], 'L1_gnn_b1a': _L1_gnn_in['b1a'], 'L1_gnn_W1b': _L1_gnn_in['W1b'], 'L1_gnn_b1b': _L1_gnn_in['b1b'], 'L1_gnn_W2a': _L1_gnn_in['W2a'], 'L1_gnn_b2a': _L1_gnn_in['b2a'], 'L1_gnn_W2b': _L1_gnn_in['W2b'], 'L1_gnn_b2b': _L1_gnn_in['b2b']}

def reference(x, src, dst, edge_attr_128, edge_weight1, L0_gnn_W1, L0_gnn_root1, L0_gnn_b1, L0_gnn_W2, L0_gnn_root2, L0_gnn_b2, L1_gnn_u, L1_gnn_W1a, L1_gnn_b1a, L1_gnn_W1b, L1_gnn_b1b, L1_gnn_W2a, L1_gnn_b2a, L1_gnn_W2b, L1_gnn_b2b):
    import jax
    import jax.numpy as jnp

    def _L0_gnn_ref(x, edge_index, pseudo, W1, root1, b1, W2, root2, b2):
        import jax, jax.numpy as jnp
        import numpy as np
        N, E, D = (50000, 18750, 128)

        def spline_conv(x, src, dst, u, W, root, bias):
            n = x.shape[0]
            h = jnp.einsum('nd,kdo->kno', x, W)
            msg = (1.0 - u)[:, None] * h[0][src] + u[:, None] * h[1][src]
            agg = jax.ops.segment_sum(msg, dst, num_segments=n)
            cnt = jax.ops.segment_sum(jnp.ones_like(u), dst, num_segments=n)
            agg = agg / jnp.maximum(cnt, 1.0)[:, None]
            return agg + x @ root + bias
        src, dst = (edge_index[0], edge_index[1])
        u = pseudo[:, 0]
        x = spline_conv(x, src, dst, u, W1, root1, b1)
        x = spline_conv(x, src, dst, u, W2, root2, b2)
        return x

    def _L1_gnn_ref(x, edge_index, edge_attr, u, batch, W1a, b1a, W1b, b1b, W2a, b2a, W2b, b2b):
        import jax, jax.numpy as jnp
        import numpy as np
        N_NODES = 50000
        N_EDGES = 18750
        D = 128
        N_GRAPHS = 64
        row, col = (edge_index[0], edge_index[1])
        h = jnp.concatenate([x[row], edge_attr], axis=1)
        h = jax.nn.relu(h @ W1a + b1a) @ W1b + b1b
        s = jax.ops.segment_sum(h, col, num_segments=x.shape[0])
        cnt = jax.ops.segment_sum(jnp.ones((col.shape[0],), x.dtype), col, num_segments=x.shape[0])
        agg = s / jnp.maximum(cnt, 1.0)[:, None]
        h2 = jnp.concatenate([x, agg, u[batch]], axis=1)
        return jax.nn.relu(h2 @ W2a + b2a) @ W2b + b2b
    edge_index = jnp.stack([src, dst])
    batch0 = jnp.zeros((50000,), jnp.int32)
    x = _layernorm(x + _L0_gnn_ref(x, edge_index, edge_weight1, L0_gnn_W1, L0_gnn_root1, L0_gnn_b1, L0_gnn_W2, L0_gnn_root2, L0_gnn_b2), axis=-1)
    x = _layernorm(x + _L1_gnn_ref(x, edge_index, edge_attr_128, L1_gnn_u, batch0, L1_gnn_W1a, L1_gnn_b1a, L1_gnn_W1b, L1_gnn_b1b, L1_gnn_W2a, L1_gnn_b2a, L1_gnn_W2b, L1_gnn_b2b), axis=-1)
    return x

_drawn_inputs = setup_inputs


def setup_inputs(seed=0):
    import zlib

    import numpy as np

    out = dict(_drawn_inputs(seed))
    spreads = {'L0_gnn_b1': (0.0, 0.1),
     'L0_gnn_b2': (0.0, 0.1),
     'L1_gnn_b1a': (0.0, 0.603),
     'L1_gnn_b1b': (0.0, 0.374),
     'L1_gnn_b2a': (0.0, 0.1),
     'L1_gnn_b2b': (0.0, 0.1)}
    factors = {}
    for name, (base, spread) in spreads.items():
        noise = np.random.default_rng([zlib.crc32(name.encode()), seed]).standard_normal(out[name].shape)
        drawn = base * np.exp(spread * noise) if base else spread * noise
        out[name] = jnp.asarray(drawn.astype(out[name].dtype))
    for name, factor in factors.items():
        out[name] = (out[name] * factor).astype(out[name].dtype)
    return out
```

```python
from contextlib import ExitStack

import concourse.bass as bass
from concourse import mybir
from concourse.bass import IndirectOffsetOnAxis

ALU = mybir.AluOpType
ACT = mybir.ActivationFunctionType
F32 = mybir.dt.float32
BF16 = mybir.dt.bfloat16
I32 = mybir.dt.int32

P = 128
U = 4
GROUP = P * U
D = 128
H = 256
COUNT = D
DEST = D + 1
ROW = D + 2
EPS = 1e-5
UNROLL = 4
LEAD = 8
NO_NODE = -1.0


class Group:

    def __init__(self, i, c, count):
        self.i, self.c, self.count = i, c, count
        self.static = isinstance(i, int)

    @property
    def number(self):
        return self.i * UNROLL + self.c

    def real(self):
        return not self.static or 0 <= self.number < self.count

    def back(self, n):
        return Group(self.i, self.c - n, self.count)

    def slot(self, slots):
        return self.c % slots

    def turn(self, slots):
        return self.i * (UNROLL // slots) + self.c // slots

    def follows(self, n):
        return not self.static or self.number >= n

    def done(self, per_group):
        return self.number * per_group + per_group

    def landed(self, per_group, slots):
        return self.turn(slots) * per_group + per_group

    def base(self, rows):
        if self.static:
            return min(GROUP * self.number, rows - GROUP)
        return self.i * (UNROLL * GROUP) + GROUP * self.c


def run_steps(eng, count, depth, step):
    turns = (count - 1 - LEAD) // UNROLL
    for c in range(LEAD):
        step(Group(0, c, count))
    first = LEAD // UNROLL
    with eng.Fori(first, first + turns) as i:
        for c in range(UNROLL):
            step(Group(i, c, count))
    for c in range(LEAD + turns * UNROLL, count + depth):
        step(Group(0, c, count))



def build(nc, x, src, dst, edge_attr, edge_weight, W1, root1, b1, W2, root2, b2,
          u_glob, W1a, b1a, W1b, b1b, W2a, b2a, W2b, b2b, out):
    N, E = x.shape[0], src.shape[0]
    NODE_GROUPS = -(-N // GROUP)
    EDGE_GROUPS = -(-E // GROUP)
    NT = NODE_GROUPS * U
    FIRST_LAST = N - GROUP
    NEW_IN_LAST = GROUP * (EDGE_GROUPS - 1) - (E - GROUP)
    assert NEW_IN_LAST % U == 0

    ctx = ExitStack()
    with ctx:
        def sb(name, shape, dt=F32):
            return ctx.enter_context(nc.sbuf_tensor(name, shape, dt))

        def pb(name, shape, dt=F32):
            return ctx.enter_context(nc.psum_tensor(name, shape, dt))

        def sem(name):
            return ctx.enter_context(nc.semaphore(name))

        def sems(name, n):
            return [sem(f"{name}{k}") for k in range(n)]

        x1_tab = nc.dram_tensor("x1_tab", (N, D), F32).ap()
        z_tab = nc.dram_tensor("z_tab", (N, D), F32).ap()
        y_tab = nc.dram_tensor("y_tab", (N, D), F32).ap()
        messages = [nc.dram_tensor(f"messages{k}", (E + P, ROW), F32).ap() for k in range(3)]

        ident = sb("ident", [P, P])
        node_iota = sb("node_iota", [P, P])
        starts = sb("starts", [P, NT])
        count_w = sb("count_w", [P, 2], BF16)
        start_row = sb("start_row", [1, NT], I32)
        inv_count = sb("inv_count", [P, NT])
        pad_rows = sb("pad_rows", [P, ROW])
        eps = sb("eps", [P, 1])
        w1 = sb("w1", [P, 2, D])
        w2 = sb("w2", [P, 2, D])
        r1 = sb("r1", [P, D])
        r2 = sb("r2", [P, D])
        w1a = sb("w1a", [P, 2, H])
        w1b = sb("w1b", [P, 2, D])
        w2a = sb("w2a", [P, 3, H])
        w2b = sb("w2b", [P, 2, D])
        b1_bc = sb("b1_bc", [P, D])
        b2_bc = sb("b2_bc", [P, D])
        b1b_bc = sb("b1b_bc", [P, D])
        b2b_bc = sb("b2b_bc", [P, D])
        b1a_col = sb("b1a_col", [P, 2])
        b2a_col = sb("b2a_col", [P, 2])
        c2_col = sb("c2_col", [P, 2])
        u_col = sb("u_col", [P, 1])

        src_t = sb("src_t", [P, 4, U], I32)
        dst_t = sb("dst_t", [P, 4, U], I32)
        u_t = sb("u_t", [P, 4, U])
        omu = sb("omu", [P, 2, U])
        below = sb("below", [P, 2, U, NT], BF16)
        rows = sb("rows", [P, 4, U, D])
        rowsT = sb("rowsT", [P, 4, GROUP])
        attr = sb("attr", [P, 2, U, D])
        attrT = sb("attrT", [P, 2, GROUP])
        hidT = sb("hidT", [P, 2, 2, GROUP])
        part0 = sb("part0", [P, 2, U, D])
        mess = sb("mess", [P, 2, U, ROW])
        window = sb("window", [P, 2, U, ROW])
        onehot = sb("onehot", [P, 2, U, P])
        agg = sb("agg", [P, 2, U, D])
        aggT = sb("aggT", [P, 2, GROUP])
        cnt = sb("cnt", [P, 2, U])
        res = sb("res", [P, 4, U, D])
        val = sb("val", [P, 2, U, D])
        stats = sb("stats", [P, 2, U, 6])
        mv = sb("mv", [P, 2, U, 2])
        std = sb("std", [P, 2, U])
        rstd = sb("rstd", [P, 2, U])
        nmr = sb("nmr", [P, 2, U])
        done = sb("done", [P, 2, U, D])

        bank = [pb(f"bank{k}", [P, GROUP]) for k in range(8)]

        def tiles(b):
            return b[:, :].rearrange("p (u f) -> p u f", u=U)

        s_w = sem("weights_loaded")
        s_pad = sem("pad_made")
        s_padst = sem("pad_stored")
        s_c0 = sem("const_filled")
        s_c1 = sem("const_ready")
        s_c2 = sem("glob_product")
        s_c2d = sem("glob_added")
        with nc.Block() as block:
            @block.sync
            def _(sp):
                for t, w in ((w1[:, :, :], W1.rearrange("k d o -> d k o")), (w2[:, :, :], W2.rearrange("k d o -> d k o")),
                             (r1[:, :], root1), (r2[:, :], root2),
                             (w1a[:, :, :], W1a.rearrange("(k p) n -> p k n", p=P)),
                             (w1b[:, :, :], W1b.rearrange("(k p) n -> p k n", p=P)),
                             (w2a[:, :, :], W2a.rearrange("(k p) n -> p k n", p=P)),
                             (w2b[:, :, :], W2b.rearrange("(k p) n -> p k n", p=P)),
                             (b1_bc[:, :], b1.partition_broadcast(P)), (b2_bc[:, :], b2.partition_broadcast(P)),
                             (b1b_bc[:, :], b1b.partition_broadcast(P)), (b2b_bc[:, :], b2b.partition_broadcast(P))):
                    sp.dma_start(t, w).then_inc(s_w, 16)
                sp.dma_start(b1a_col[:, :], b1a.rearrange("(m p) -> p m", p=P), allow_slow_non_contiguous=True).then_inc(s_w, 16)
                sp.dma_start(b2a_col[:, :], b2a.rearrange("(m p) -> p m", p=P), allow_slow_non_contiguous=True).then_inc(s_w, 16)
                sp.dma_start(u_col[:, :], u_glob[0:1, :].rearrange("a p -> p a"), allow_slow_non_contiguous=True).then_inc(s_w, 16)
                sp.wait_ge(s_pad, 2)
                for m in messages:
                    sp.dma_start(m[E:E + P, :], pad_rows[:, :]).then_inc(s_padst, 16)
                sp.wait_ge(s_padst, 16 * len(messages))
                sp.wait_ge(s_w, 16 * 15)

            @block.gpsimd
            def _(pool):
                pool.memset(ident[:, :], 0.0).then_inc(s_c0, 1)
                pool.memset(count_w[:, :], 1.0).then_inc(s_c0, 1)
                pool.iota(node_iota[:, :], [[1, P]], base=0, channel_multiplier=0, allow_small_or_imprecise_dtypes=True)
                pool.iota(starts[:, 0:NT - U], [[P, NT - U]], base=0, channel_multiplier=0, allow_small_or_imprecise_dtypes=True)
                pool.iota(starts[:, NT - U:NT], [[P, U]], base=FIRST_LAST, channel_multiplier=0, allow_small_or_imprecise_dtypes=True)
                pool.wait_ge(s_c0, 2)
                pool.affine_select(out=ident[:, :], in_=ident[:, :], compare_op=ALU.not_equal, fill=1.0,
                                   base=0, pattern=[[-1, P]], channel_multiplier=1)
                pool.affine_select(out=count_w[:, 1:2], in_=count_w[:, 1:2], compare_op=ALU.is_ge, fill=0.0,
                                   base=-(NEW_IN_LAST // U), pattern=[[0, 1]], channel_multiplier=1).then_inc(s_c1, 1)

            @block.tensor
            def _(pe):
                pe.wait_ge(s_w, 16 * 15)
                for m in range(2):
                    mm = pe.matmul(bank[0][:, m:m + 1], w2a[:, 2, m * P:(m + 1) * P], u_col[:, :], start=True, stop=True)
                mm.then_inc(s_c2, 1)

            @block.vector
            def _(dve):
                dve.memset(pad_rows[:, 0:DEST], 0.0).then_inc(s_pad, 1)
                dve.memset(pad_rows[:, DEST:ROW], NO_NODE).then_inc(s_pad, 1)
                dve.memset(mess[:, :, :, COUNT:COUNT + 1], 1.0)
                dve.memset(eps[:, :], EPS)
                dve.wait_ge(s_c2, 1)
                dve.tensor_tensor(c2_col[:, :], bank[0][:, 0:2], b2a_col[:, :], ALU.add).then_inc(s_c2d, 1)

        def edge_conv(name, table, w, out_rows, counting):
            s_idx = sems(name + "_edges_loaded", 4)
            s_got = sems(name + "_rows_gathered", 4)
            s_go = sem(name + "_gather_released")
            s_put = sems(name + "_messages_stored", 2)
            s_T = sem(name + "_rows_transposed")
            s_xT = sem(name + "_rowsT_copied")
            s_mm = sem(name + "_products")
            s_om = sem(name + "_omu_ready")
            s_df = sem(name + "_dest_ready")
            s_t0 = sem(name + "_part0_ready")
            s_ms = sem(name + "_messages_ready")
            s_bl = sem(name + "_below_ready")
            s_ct = sem(name + "_below_summed")
            with nc.Block() as block:
                @block.sync
                def _(sp):
                    def step(s):
                        if s.real():
                            g = s
                            at = sp.snap(g.base(E)) if not g.static else g.base(E)
                            if g.follows(4):
                                sp.wait_ge(s_ms, g.back(4).done(1))
                            k = g.slot(4)
                            for t, v in ((src_t, src), (dst_t, dst), (u_t, edge_weight)):
                                sp.dma_start(t[:, k, :], v[bass.ds(at, GROUP)].rearrange("(p u) -> p u", u=U)).then_inc(s_idx[k], 16)
                        g = s.back(3)
                        if g.real():
                            at = sp.snap(g.base(E)) if not g.static else g.base(E)
                            sp.wait_ge(s_ms, g.done(1))
                            if g.static and g.number == EDGE_GROUPS - 1:
                                if g.follows(1):
                                    sp.wait_ge(s_put[g.back(1).slot(2)], g.back(1).landed(16, 2))
                            sp.dma_start(out_rows[bass.ds(at, GROUP), :].rearrange("(p u) f -> p u f", u=U),
                                         mess[:, g.slot(2), :, :]).then_inc(s_put[g.slot(2)], 16)
                    run_steps(sp, EDGE_GROUPS, 3, step)
                    sp.wait_ge(s_put[Group(0, EDGE_GROUPS - 1, EDGE_GROUPS).slot(2)], Group(0, EDGE_GROUPS - 1, EDGE_GROUPS).landed(16, 2))
                    sp.wait_ge(s_put[Group(0, EDGE_GROUPS - 2, EDGE_GROUPS).slot(2)], Group(0, EDGE_GROUPS - 2, EDGE_GROUPS).landed(16, 2))

                @block.gpsimd
                def _(pool):
                    top = pool.to_reg(N - 1)

                    def step(g):
                        if g.real():
                            pool.wait_ge(s_idx[g.slot(4)], g.landed(48, 4))
                            if g.follows(4):
                                pool.wait_ge(s_T, g.back(4).done(1))
                            pool.sem_inc(s_go, 1)
                            for t in range(U):
                                pool.indirect_dma_start(rows[:, g.slot(4), t, :], None, table,
                                                        IndirectOffsetOnAxis(ap=src_t[:, g.slot(4), t:t + 1], axis=0),
                                                        bounds_check=top, oob_is_err=False).then_inc(s_got[g.slot(4)], 16)
                    run_steps(pool, EDGE_GROUPS, 0, step)

                @block.tensor
                def _(pe):
                    def step(s):
                        if s.real():
                            g = s
                            if g.follows(1):
                                pe.wait_ge(s_xT, g.back(1).done(1))
                            pe.wait_ge(s_got[g.slot(4)], g.landed(16 * U, 4))
                            for t in range(U):
                                mm = pe.transpose(tiles(bank[0])[:, t, :], rows[:, g.slot(4), t, :], ident[:, :])
                            mm.then_inc(s_T, 1)
                        g = s.back(1)
                        if g.real():
                            pe.wait_ge(s_xT, g.done(1))
                            if g.follows(2):
                                pe.wait_ge(s_ms, g.back(2).done(1))
                            for t in range(U):
                                b = bank[1 + 2 * g.slot(2) + t // 2]
                                mm = pe.matmul(b[:, (t % 2) * 2 * D:(t % 2 + 1) * 2 * D], rowsT[:, g.slot(2), t * P:(t + 1) * P],
                                               w[:, :, :].rearrange("p k o -> p (k o)"), start=True, stop=True)
                            mm.then_inc(s_mm, 1)
                            if counting:
                                pe.wait_ge(s_bl, g.done(1))
                                last = g.static and g.number == EDGE_GROUPS - 1
                                for t in range(U):
                                    mm = pe.matmul(bank[5][0:1, 0:NT], count_w[:, int(last):int(last) + 1], below[:, g.slot(2), t, :],
                                                   start=(g.static and g.number == 0 and t == 0), stop=(last and t == U - 1))
                                mm.then_inc(s_ct, 1)
                    run_steps(pe, EDGE_GROUPS, 1, step)

                @block.scalar
                def _(act):
                    def step(s):
                        if s.real():
                            g = s
                            if g.follows(2):
                                act.wait_ge(s_mm, g.back(2).done(1))
                            act.wait_ge(s_T, g.done(1))
                            act.activation(rowsT[:, g.slot(2), :], bank[0][:, :], ACT.Copy).then_inc(s_xT, 1)
                        g = s.back(1)
                        if g.real():
                            act.wait_ge(s_om, g.done(1))
                            if g.follows(2):
                                act.wait_ge(s_ms, g.back(2).done(1))
                            act.wait_ge(s_mm, g.done(1))
                            for t in range(U):
                                b = bank[1 + 2 * g.slot(2) + t // 2]
                                a = act.activation(part0[:, g.slot(2), t, :], b[:, (t % 2) * 2 * D:(t % 2) * 2 * D + D], ACT.Copy,
                                                   scale=omu[:, g.slot(2), t:t + 1])
                            a.then_inc(s_t0, 1)
                    run_steps(act, EDGE_GROUPS, 1, step)

                @block.vector
                def _(dve):
                    def step(s):
                        if s.real():
                            g = s
                            if g.follows(2):
                                dve.wait_ge(s_t0, g.back(2).done(1))
                            dve.wait_ge(s_idx[g.slot(4)], g.landed(48, 4))
                            dve.tensor_scalar(omu[:, g.slot(2), :], u_t[:, g.slot(4), :], -1.0, 1.0, ALU.mult, ALU.add).then_inc(s_om, 1)
                            if g.follows(2):
                                dve.wait_ge(s_put[g.back(2).slot(2)], g.back(2).landed(16, 2))
                            dve.tensor_copy(mess[:, g.slot(2), :, DEST:ROW].rearrange("p u a -> p (u a)"), dst_t[:, g.slot(4), :]).then_inc(s_df, 1)
                            if counting:
                                if g.follows(2):
                                    dve.wait_ge(s_ct, g.back(2).done(1))
                                dve.wait_ge(s_df, g.done(1))
                                for t in range(U):
                                    d = dve.tensor_scalar(below[:, g.slot(2), t, :], starts[:, :], mess[:, g.slot(2), t, DEST:ROW],
                                                          None, ALU.is_gt)
                                d.then_inc(s_bl, 1)
                        g = s.back(1)
                        if g.real():
                            dve.wait_ge(s_t0, g.done(1))
                            for t in range(U):
                                b = bank[1 + 2 * g.slot(2) + t // 2]
                                d = dve.scalar_tensor_tensor(out=mess[:, g.slot(2), t, 0:D], in0=b[:, (t % 2) * 2 * D + D:(t % 2 + 1) * 2 * D],
                                                             scalar=u_t[:, g.slot(4), t:t + 1], in1=part0[:, g.slot(2), t, :],
                                                             op0=ALU.mult, op1=ALU.add)
                            d.then_inc(s_ms, 1)
                    run_steps(dve, EDGE_GROUPS, 1, step)
                    if counting:
                        dve.wait_ge(s_ct, EDGE_GROUPS)
                        dve.tensor_copy(start_row[:, :], bank[5][0:1, 0:NT])

        def edge_mlp(name, table, out_rows):
            s_idx = sems(name + "_edges_loaded", 4)
            s_at = sems(name + "_attributes_loaded", 2)
            s_got = sems(name + "_rows_gathered", 4)
            s_go = sem(name + "_gather_released")
            s_put = sems(name + "_messages_stored", 2)
            s_T = sem(name + "_rows_transposed")
            s_aT = sem(name + "_attributes_transposed")
            s_xTc = sem(name + "_rowsT_copied")
            s_aTc = sem(name + "_attrT_copied")
            s_h = sem(name + "_hidden_products")
            s_hr = sem(name + "_hidden_ready")
            s_o = sem(name + "_outputs_products")
            s_df = sem(name + "_dest_ready")
            s_ms = sem(name + "_messages_ready")
            with nc.Block() as block:
                @block.sync
                def _(sp):
                    def step(s):
                        if s.real():
                            g = s
                            at = sp.snap(g.base(E)) if not g.static else g.base(E)
                            if g.follows(4):
                                sp.wait_ge(s_ms, g.back(4).done(1))
                            k = g.slot(4)
                            for t, v in ((src_t, src), (dst_t, dst)):
                                sp.dma_start(t[:, k, :], v[bass.ds(at, GROUP)].rearrange("(p u) -> p u", u=U)).then_inc(s_idx[k], 16)
                            if g.follows(2):
                                sp.wait_ge(s_aT, g.back(2).done(1))
                            sp.dma_start(attr[:, g.slot(2), :, :],
                                         edge_attr[bass.ds(at, GROUP), :].rearrange("(p u) f -> p u f", u=U)).then_inc(s_at[g.slot(2)], 16)
                        g = s.back(4)
                        if g.real():
                            at = sp.snap(g.base(E)) if not g.static else g.base(E)
                            sp.wait_ge(s_ms, g.done(1))
                            if g.static and g.number == EDGE_GROUPS - 1:
                                if g.follows(1):
                                    sp.wait_ge(s_put[g.back(1).slot(2)], g.back(1).landed(16, 2))
                            sp.dma_start(out_rows[bass.ds(at, GROUP), :].rearrange("(p u) f -> p u f", u=U),
                                         mess[:, g.slot(2), :, :]).then_inc(s_put[g.slot(2)], 16)
                    run_steps(sp, EDGE_GROUPS, 4, step)
                    sp.wait_ge(s_put[Group(0, EDGE_GROUPS - 1, EDGE_GROUPS).slot(2)], Group(0, EDGE_GROUPS - 1, EDGE_GROUPS).landed(16, 2))
                    sp.wait_ge(s_put[Group(0, EDGE_GROUPS - 2, EDGE_GROUPS).slot(2)], Group(0, EDGE_GROUPS - 2, EDGE_GROUPS).landed(16, 2))

                @block.gpsimd
                def _(pool):
                    top = pool.to_reg(N - 1)

                    def step(g):
                        if g.real():
                            pool.wait_ge(s_idx[g.slot(4)], g.landed(32, 4))
                            if g.follows(4):
                                pool.wait_ge(s_T, g.back(4).done(1))
                            pool.sem_inc(s_go, 1)
                            for t in range(U):
                                pool.indirect_dma_start(rows[:, g.slot(4), t, :], None, table,
                                                        IndirectOffsetOnAxis(ap=src_t[:, g.slot(4), t:t + 1], axis=0),
                                                        bounds_check=top, oob_is_err=False).then_inc(s_got[g.slot(4)], 16)
                    run_steps(pool, EDGE_GROUPS, 0, step)

                @block.tensor
                def _(pe):
                    def step(s):
                        if s.real():
                            g = s
                            if g.follows(1):
                                pe.wait_ge(s_aTc, g.back(1).done(1))
                            pe.wait_ge(s_at[g.slot(2)], g.landed(16, 2))
                            for t in range(U):
                                mm = pe.transpose(tiles(bank[1])[:, t, :], attr[:, g.slot(2), t, :], ident[:, :])
                            mm.then_inc(s_aT, 1)
                            if g.follows(1):
                                pe.wait_ge(s_xTc, g.back(1).done(1))
                            pe.wait_ge(s_got[g.slot(4)], g.landed(16 * U, 4))
                            for t in range(U):
                                mm = pe.transpose(tiles(bank[0])[:, t, :], rows[:, g.slot(4), t, :], ident[:, :])
                            mm.then_inc(s_T, 1)
                        g = s.back(1)
                        if g.real():
                            pe.wait_ge(s_aTc, g.done(1))
                            pe.wait_ge(s_xTc, g.done(1))
                            if g.follows(1):
                                pe.wait_ge(s_hr, g.back(1).done(2))
                            for m in range(2):
                                h = bank[2 + m]
                                pe.matmul(h[:, :], w1a[:, 1, m * P:(m + 1) * P], attrT[:, g.slot(2), :], start=True, stop=False)
                                pe.matmul(h[:, :], w1a[:, 0, m * P:(m + 1) * P], rowsT[:, g.slot(2), :], start=False, stop=True).then_inc(s_h, 1)
                        g = s.back(2)
                        if g.real():
                            pe.wait_ge(s_hr, g.done(2))
                            if g.follows(1):
                                pe.wait_ge(s_ms, g.back(1).done(1))
                            for t in range(U):
                                pe.matmul(tiles(bank[4])[:, t, :], hidT[:, g.slot(2), 0, t * P:(t + 1) * P], w1b[:, 0, :], start=True, stop=False)
                                mm = pe.matmul(tiles(bank[4])[:, t, :], hidT[:, g.slot(2), 1, t * P:(t + 1) * P], w1b[:, 1, :], start=False, stop=True)
                            mm.then_inc(s_o, 1)
                    run_steps(pe, EDGE_GROUPS, 2, step)

                @block.scalar
                def _(act):
                    def step(s):
                        if s.real():
                            g = s
                            if g.follows(2):
                                act.wait_ge(s_h, g.back(2).done(2))
                            act.wait_ge(s_T, g.done(1))
                            act.activation(rowsT[:, g.slot(2), :], bank[0][:, :], ACT.Copy).then_inc(s_xTc, 1)
                        g = s.back(1)
                        if g.real():
                            if g.follows(2):
                                act.wait_ge(s_o, g.back(2).done(1))
                            for m in range(2):
                                act.wait_ge(s_h, g.number * 2 + (m + 1))
                                act.activation(hidT[:, g.slot(2), m, :], bank[2 + m][:, :], ACT.Relu, bias=b1a_col[:, m:m + 1]).then_inc(s_hr, 1)
                    run_steps(act, EDGE_GROUPS, 1, step)

                @block.vector
                def _(dve):
                    def step(s):
                        if s.real():
                            g = s
                            if g.follows(2):
                                dve.wait_ge(s_h, g.back(2).done(2))
                            dve.wait_ge(s_aT, g.done(1))
                            dve.tensor_copy(attrT[:, g.slot(2), :], bank[1][:, :]).then_inc(s_aTc, 1)
                        g = s.back(2)
                        if g.real():
                            dve.wait_ge(s_idx[g.slot(4)], g.landed(32, 4))
                            if g.follows(2):
                                dve.wait_ge(s_put[g.back(2).slot(2)], g.back(2).landed(16, 2))
                            dve.tensor_copy(mess[:, g.slot(2), :, DEST:ROW].rearrange("p u a -> p (u a)"), dst_t[:, g.slot(4), :])
                            dve.wait_ge(s_o, g.done(1))
                            for t in range(U):
                                d = dve.tensor_tensor(mess[:, g.slot(2), t, 0:D], tiles(bank[4])[:, t, :], b1b_bc[:, :], ALU.add)
                            d.then_inc(s_ms, 1)
                    run_steps(dve, EDGE_GROUPS, 2, step)

        def load_windows(sp, g, table, s_win, regs):
            sp.load(regs, start_row[0:1, bass.ds(g.number * U, U)])
            for t in range(U):
                at = sp.snap(regs[t], min_val=0, max_val=E)
                sp.dma_start(window[:, g.slot(2), t, :], table[bass.ds(at, P), :]).then_inc(s_win[g.slot(2)], 16)

        def make_onehot(dve, g, s_oh, s_ag, s_win):
            if g.follows(2):
                dve.wait_ge(s_ag, g.back(2).done(1))
            dve.wait_ge(s_win[g.slot(2)], g.landed(16 * U, 2))
            for t in range(U):
                tile = g.number * U + t
                d = dve.tensor_scalar(onehot[:, g.slot(2), t, :], node_iota[:, :], starts[:, bass.ds(tile, 1)],
                                      window[:, g.slot(2), t, DEST:ROW], ALU.add, ALU.is_equal)
            d.then_inc(s_oh, 1)

        def node_rows(table, at):
            return table[bass.ds(at, GROUP), :].rearrange("(u p) f -> p u f", p=P)

        def node_first(name, table):
            s_x = sems(name + "_x_loaded", 4)
            s_win = sems(name + "_windows_loaded", 2)
            s_px1 = sems(name + "_x1_stored", 2)
            s_pz = sems(name + "_z_stored", 2)
            s_T = sem(name + "_x_transposed")
            s_xT = sem(name + "_xT_copied")
            s_oh = sem(name + "_onehot_ready")
            s_ag = sem(name + "_sums")
            s_r1 = sem(name + "_root1_product")
            s_ct = sem(name + "_count_read")
            s_iv = sem(name + "_inverse_ready")
            s_me = sem(name + "_mean_ready")
            s_x1 = sem(name + "_x1_ready")
            s_T1 = sem(name + "_x1_transposed")
            s_x1T = sem(name + "_x1T_copied")
            s_r2 = sem(name + "_root2_product")
            s_xb = sem(name + "_x_plus_bias")
            s_z = sem(name + "_z_ready")
            x1 = val
            z = done
            x1T = aggT
            with nc.Block() as block:
                @block.sync
                def _(sp):
                    regs = [ctx.enter_context(sp.register(name=f"{name}_start{t}")) for t in range(U)]

                    def step(s):
                        if s.real():
                            g = s
                            at = sp.snap(g.base(N)) if not g.static else g.base(N)
                            if g.follows(4):
                                sp.wait_ge(s_T, g.back(4).done(1))
                            if g.follows(4):
                                sp.wait_ge(s_xb, g.back(4).done(1))
                            sp.dma_start(rows[:, g.slot(4), :, :], node_rows(x, at)).then_inc(s_x[g.slot(4)], 16)
                            if g.follows(2):
                                sp.wait_ge(s_ag, g.back(2).done(1))
                            load_windows(sp, g, table, s_win, regs)
                        for k, s_ready, s_put, t, tab in ((3, s_x1, s_px1, x1, x1_tab), (4, s_z, s_pz, z, z_tab)):
                            g = s.back(k)
                            if g.real():
                                at = sp.snap(g.base(N)) if not g.static else g.base(N)
                                sp.wait_ge(s_ready, g.done(1))
                                if g.static and g.number == NODE_GROUPS - 1:
                                    if g.follows(1):
                                        sp.wait_ge(s_put[g.back(1).slot(2)], g.back(1).landed(16, 2))
                                sp.dma_start(node_rows(tab, at), t[:, g.slot(2), :, :]).then_inc(s_put[g.slot(2)], 16)
                    run_steps(sp, NODE_GROUPS, 4, step)
                    for s_put in (s_px1, s_pz):
                        sp.wait_ge(s_put[Group(0, NODE_GROUPS - 1, NODE_GROUPS).slot(2)], Group(0, NODE_GROUPS - 1, NODE_GROUPS).landed(16, 2))
                        sp.wait_ge(s_put[Group(0, NODE_GROUPS - 2, NODE_GROUPS).slot(2)], Group(0, NODE_GROUPS - 2, NODE_GROUPS).landed(16, 2))

                @block.gpsimd
                def _(pool):
                    def step(g):
                        if g.real():
                            if g.follows(4):
                                pool.wait_ge(s_z, g.back(4).done(1))
                            pool.wait_ge(s_x[g.slot(4)], g.landed(16, 4))
                            for t in range(U):
                                p = pool.tensor_tensor(res[:, g.slot(4), t, :], rows[:, g.slot(4), t, :], b2_bc[:, :], ALU.add)
                            p.then_inc(s_xb, 1)
                    run_steps(pool, NODE_GROUPS, 0, step)

                @block.tensor
                def _(pe):
                    def step(s):
                        if s.real():
                            g = s
                            if g.follows(1):
                                pe.wait_ge(s_xT, g.back(1).done(1))
                            pe.wait_ge(s_x[g.slot(4)], g.landed(16, 4))
                            for t in range(U):
                                mm = pe.transpose(tiles(bank[0])[:, t, :], rows[:, g.slot(4), t, :], ident[:, :])
                            mm.then_inc(s_T, 1)
                        g = s.back(1)
                        if g.real():
                            pe.wait_ge(s_xT, g.done(1))
                            if g.follows(1):
                                pe.wait_ge(s_x1, g.back(1).done(1))
                            for t in range(U):
                                mm = pe.matmul(tiles(bank[1])[:, t, :], rowsT[:, g.slot(2), t * P:(t + 1) * P], r1[:, :], start=True, stop=True)
                            mm.then_inc(s_r1, 1)
                        g = s.back(3)
                        if g.real():
                            pe.wait_ge(s_x1T, g.done(1))
                            if g.follows(1):
                                pe.wait_ge(s_z, g.back(1).done(1))
                            for t in range(U):
                                mm = pe.matmul(tiles(bank[5])[:, t, :], x1T[:, g.slot(2), t * P:(t + 1) * P], r2[:, :], start=True, stop=True)
                            mm.then_inc(s_r2, 1)
                        g = s.back(2)
                        if g.real():
                            if g.follows(1):
                                pe.wait_ge(s_x1T, g.back(1).done(1))
                            pe.wait_ge(s_x1, g.done(1))
                            for t in range(U):
                                mm = pe.transpose(tiles(bank[4])[:, t, :], x1[:, g.slot(2), t, :], ident[:, :])
                            mm.then_inc(s_T1, 1)
                        g = s
                        if g.real():
                            pe.wait_ge(s_oh, g.done(1))
                            if g.follows(1):
                                pe.wait_ge(s_me, g.back(1).done(1))
                            for t in range(U):
                                mm = pe.matmul(bank[2 + t // 2][:, (t % 2) * 256:(t % 2) * 256 + D + 1], onehot[:, g.slot(2), t, :],
                                               window[:, g.slot(2), t, 0:D + 1], start=True, stop=True)
                            mm.then_inc(s_ag, 1)
                    run_steps(pe, NODE_GROUPS, 3, step)

                @block.scalar
                def _(act):
                    def step(s):
                        if s.real():
                            g = s
                            if g.follows(2):
                                act.wait_ge(s_r1, g.back(2).done(1))
                            act.wait_ge(s_T, g.done(1))
                            act.activation(rowsT[:, g.slot(2), :], bank[0][:, :], ACT.Copy).then_inc(s_xT, 1)
                        g = s.back(2)
                        if g.real():
                            if g.follows(2):
                                act.wait_ge(s_r2, g.back(2).done(1))
                            act.wait_ge(s_T1, g.done(1))
                            act.activation(x1T[:, g.slot(2), :], bank[4][:, :], ACT.Copy).then_inc(s_x1T, 1)
                    run_steps(act, NODE_GROUPS, 2, step)

                @block.vector
                def _(dve):
                    def step(s):
                        if s.real():
                            make_onehot(dve, s, s_oh, s_ag, s_win)
                        g = s.back(1)
                        if g.real():
                            dve.wait_ge(s_ag, g.done(1))
                            for b in range(2):
                                d = dve.tensor_scalar(cnt[:, g.slot(2), 2 * b:2 * b + 2], bank[2 + b][:, D::256], 1.0, None, ALU.max)
                            d.then_inc(s_ct, 1)
                            dve.wait_ge(s_ct, g.done(1))
                            dve.reciprocal(inv_count[:, bass.ds(g.number * U, U)], cnt[:, g.slot(2), :]).then_inc(s_iv, 1)
                            dve.wait_ge(s_iv, g.done(1))
                            for t in range(U):
                                d = dve.scalar_tensor_tensor(out=agg[:, g.slot(2), t, :], in0=bank[2 + t // 2][:, (t % 2) * 256:(t % 2) * 256 + D],
                                                             scalar=inv_count[:, bass.ds(g.number * U + t, 1)], in1=b1_bc[:, :],
                                                             op0=ALU.mult, op1=ALU.add)
                            d.then_inc(s_me, 1)
                        g = s.back(3)
                        if g.real():
                            if g.follows(2):
                                dve.wait_ge(s_pz[g.back(2).slot(2)], g.back(2).landed(16, 2))
                            dve.wait_ge(s_xb, g.done(1))
                            dve.wait_ge(s_r2, g.done(1))
                            dve.tensor_tensor(z[:, g.slot(2), :, :], tiles(bank[5]), res[:, g.slot(4), :, :], ALU.add).then_inc(s_z, 1)
                        g = s.back(1)
                        if g.real():
                            if g.follows(2):
                                dve.wait_ge(s_px1[g.back(2).slot(2)], g.back(2).landed(16, 2))
                            if g.follows(2):
                                dve.wait_ge(s_T1, g.back(2).done(1))
                            dve.wait_ge(s_r1, g.done(1))
                            dve.wait_ge(s_me, g.done(1))
                            dve.tensor_tensor(x1[:, g.slot(2), :, :], tiles(bank[1]), agg[:, g.slot(2), :, :], ALU.add).then_inc(s_x1, 1)
                    run_steps(dve, NODE_GROUPS, 3, step)

        class Norm:

            def __init__(self, name):
                self.s_v = sem(name + "_value_ready")
                self.s_bs = sem(name + "_stats_ready")
                self.s_go = sem(name + "_aggregation_released")
                self.s_mv = sem(name + "_moments_ready")
                self.s_sd = sem(name + "_deviation_ready")
                self.s_rs = sem(name + "_rstd_ready")
                self.s_nm = sem(name + "_shift_ready")
                self.s_y = sem(name + "_normed")

            def moments(self, dve, g):
                k = g.slot(2)
                dve.wait_ge(self.s_v, g.done(1))
                for t in range(U):
                    d = dve.bn_stats(stats[:, k, t, :], val[:, k, t, :])
                d.then_inc(self.s_bs, 1)
                if g.follows(2):
                    dve.wait_ge(self.s_sd, g.back(2).done(1))
                dve.wait_ge(self.s_bs, g.done(1))
                dve.sem_inc(self.s_go, 1)
                for t in range(U):
                    d = dve.bn_aggr(mv[:, k, t, :], stats[:, k, t, :])
                d.then_inc(self.s_mv, 1)

            def deviation(self, act, g):
                k = g.slot(2)
                act.wait_ge(self.s_mv, g.done(1))
                if g.follows(2):
                    act.wait_ge(self.s_rs, g.back(2).done(1))
                act.activation(std[:, k, :], mv[:, k, :, 1], ACT.Sqrt, bias=eps[:, :]).then_inc(self.s_sd, 1)

            def scales(self, dve, g):
                k = g.slot(2)
                dve.wait_ge(self.s_sd, g.done(1))
                if g.follows(2):
                    dve.wait_ge(self.s_y, g.back(2).done(1))
                dve.reciprocal(rstd[:, k, :], std[:, k, :]).then_inc(self.s_rs, 1)
                dve.wait_ge(self.s_rs, g.done(1))
                dve.scalar_tensor_tensor(out=nmr[:, k, :], in0=mv[:, k, :, 0], scalar=-1.0, in1=rstd[:, k, :],
                                         op0=ALU.mult, op1=ALU.mult).then_inc(self.s_nm, 1)

            def apply(self, act, g, s_put):
                k = g.slot(2)
                if g.follows(2):
                    act.wait_ge(s_put[g.back(2).slot(2)], g.back(2).landed(16, 2))
                act.wait_ge(self.s_nm, g.done(1))
                for t in range(U):
                    a = act.activation(done[:, k, t, :], val[:, k, t, :], ACT.Identity, bias=nmr[:, k, t:t + 1], scale=rstd[:, k, t:t + 1])
                a.then_inc(self.s_y, 1)

        def node_second(name, table):
            s_x = sems(name + "_z_loaded", 4)
            s_win = sems(name + "_windows_loaded", 2)
            s_put = sems(name + "_y_stored", 2)
            s_oh = sem(name + "_onehot_ready")
            s_ag = sem(name + "_sums")
            norm = Norm(name)
            with nc.Block() as block:
                @block.sync
                def _(sp):
                    regs = [ctx.enter_context(sp.register(name=f"{name}_start{t}")) for t in range(U)]

                    def step(s):
                        if s.real():
                            g = s
                            at = sp.snap(g.base(N)) if not g.static else g.base(N)
                            if g.follows(4):
                                sp.wait_ge(norm.s_v, g.back(4).done(1))
                            sp.dma_start(rows[:, g.slot(4), :, :], node_rows(z_tab, at)).then_inc(s_x[g.slot(4)], 16)
                            if g.follows(2):
                                sp.wait_ge(s_ag, g.back(2).done(1))
                            load_windows(sp, g, table, s_win, regs)
                        g = s.back(3)
                        if g.real():
                            at = sp.snap(g.base(N)) if not g.static else g.base(N)
                            sp.wait_ge(norm.s_y, g.done(1))
                            if g.static and g.number == NODE_GROUPS - 1:
                                if g.follows(1):
                                    sp.wait_ge(s_put[g.back(1).slot(2)], g.back(1).landed(16, 2))
                            sp.dma_start(node_rows(y_tab, at), done[:, g.slot(2), :, :]).then_inc(s_put[g.slot(2)], 16)
                    run_steps(sp, NODE_GROUPS, 3, step)
                    sp.wait_ge(s_put[Group(0, NODE_GROUPS - 1, NODE_GROUPS).slot(2)], Group(0, NODE_GROUPS - 1, NODE_GROUPS).landed(16, 2))
                    sp.wait_ge(s_put[Group(0, NODE_GROUPS - 2, NODE_GROUPS).slot(2)], Group(0, NODE_GROUPS - 2, NODE_GROUPS).landed(16, 2))

                @block.tensor
                def _(pe):
                    def step(g):
                        if g.real():
                            pe.wait_ge(s_oh, g.done(1))
                            if g.follows(2):
                                pe.wait_ge(norm.s_v, g.back(2).done(1))
                            for t in range(U):
                                mm = pe.matmul(tiles(bank[g.slot(2)])[:, t, :], onehot[:, g.slot(2), t, :], window[:, g.slot(2), t, 0:D],
                                               start=True, stop=True)
                            mm.then_inc(s_ag, 1)
                    run_steps(pe, NODE_GROUPS, 0, step)

                @block.scalar
                def _(act):
                    def step(s):
                        g = s.back(1)
                        if g.real():
                            norm.deviation(act, g)
                        g = s.back(2)
                        if g.real():
                            norm.apply(act, g, s_put)
                    run_steps(act, NODE_GROUPS, 2, step)

                @block.vector
                def _(dve):
                    def step(s):
                        if s.real():
                            make_onehot(dve, s, s_oh, s_ag, s_win)
                        g = s.back(2)
                        if g.real():
                            norm.scales(dve, g)
                        g = s.back(1)
                        if g.real():
                            dve.wait_ge(s_x[g.slot(4)], g.landed(16, 4))
                            if g.follows(2):
                                dve.wait_ge(norm.s_y, g.back(2).done(1))
                            dve.wait_ge(s_ag, g.done(1))
                            for t in range(U):
                                d = dve.scalar_tensor_tensor(out=val[:, g.slot(2), t, :], in0=tiles(bank[g.slot(2)])[:, t, :],
                                                             scalar=inv_count[:, bass.ds(g.number * U + t, 1)], in1=rows[:, g.slot(4), t, :],
                                                             op0=ALU.mult, op1=ALU.add)
                            d.then_inc(norm.s_v, 1)
                            norm.moments(dve, g)
                    run_steps(dve, NODE_GROUPS, 2, step)

        def node_third(name, table):
            s_x = sems(name + "_y_loaded", 4)
            s_win = sems(name + "_windows_loaded", 2)
            s_put = sems(name + "_out_stored", 2)
            s_oh = sem(name + "_onehot_ready")
            s_ag = sem(name + "_sums")
            s_T = sem(name + "_y_transposed")
            s_xT = sem(name + "_yT_copied")
            s_me = sem(name + "_means_ready")
            s_Tm = sem(name + "_means_transposed")
            s_mT = sem(name + "_meansT_copied")
            s_h = sem(name + "_hidden_products")
            s_hr = sem(name + "_hidden_ready")
            s_o = sem(name + "_out_products")
            s_xb = sem(name + "_y_plus_bias")
            norm = Norm(name)
            with nc.Block() as block:
                @block.sync
                def _(sp):
                    regs = [ctx.enter_context(sp.register(name=f"{name}_start{t}")) for t in range(U)]

                    def step(s):
                        if s.real():
                            g = s
                            at = sp.snap(g.base(N)) if not g.static else g.base(N)
                            if g.follows(4):
                                sp.wait_ge(s_T, g.back(4).done(1))
                            if g.follows(4):
                                sp.wait_ge(s_xb, g.back(4).done(1))
                            sp.dma_start(rows[:, g.slot(4), :, :], node_rows(y_tab, at)).then_inc(s_x[g.slot(4)], 16)
                            if g.follows(2):
                                sp.wait_ge(s_ag, g.back(2).done(1))
                            load_windows(sp, g, table, s_win, regs)
                        g = s.back(5)
                        if g.real():
                            at = sp.snap(g.base(N)) if not g.static else g.base(N)
                            sp.wait_ge(norm.s_y, g.done(1))
                            if g.static and g.number == NODE_GROUPS - 1:
                                if g.follows(1):
                                    sp.wait_ge(s_put[g.back(1).slot(2)], g.back(1).landed(16, 2))
                            sp.dma_start(node_rows(out, at), done[:, g.slot(2), :, :]).then_inc(s_put[g.slot(2)], 16)
                    run_steps(sp, NODE_GROUPS, 5, step)
                    sp.wait_ge(s_put[Group(0, NODE_GROUPS - 1, NODE_GROUPS).slot(2)], Group(0, NODE_GROUPS - 1, NODE_GROUPS).landed(16, 2))
                    sp.wait_ge(s_put[Group(0, NODE_GROUPS - 2, NODE_GROUPS).slot(2)], Group(0, NODE_GROUPS - 2, NODE_GROUPS).landed(16, 2))

                @block.gpsimd
                def _(pool):
                    def step(g):
                        if g.real():
                            if g.follows(4):
                                pool.wait_ge(norm.s_v, g.back(4).done(1))
                            pool.wait_ge(s_x[g.slot(4)], g.landed(16, 4))
                            for t in range(U):
                                p = pool.tensor_tensor(res[:, g.slot(4), t, :], rows[:, g.slot(4), t, :], b2b_bc[:, :], ALU.add)
                            p.then_inc(s_xb, 1)
                    run_steps(pool, NODE_GROUPS, 0, step)

                @block.tensor
                def _(pe):
                    def step(s):
                        if s.real():
                            g = s
                            if g.follows(1):
                                pe.wait_ge(s_xT, g.back(1).done(1))
                            pe.wait_ge(s_x[g.slot(4)], g.landed(16, 4))
                            for t in range(U):
                                mm = pe.transpose(tiles(bank[0])[:, t, :], rows[:, g.slot(4), t, :], ident[:, :])
                            mm.then_inc(s_T, 1)
                        g = s.back(2)
                        if g.real():
                            pe.wait_ge(s_mT, g.done(1))
                            if g.follows(1):
                                pe.wait_ge(s_hr, g.back(1).done(2))
                            for m in range(2):
                                h = bank[4 + m]
                                pe.matmul(h[:, :], w2a[:, 0, m * P:(m + 1) * P], rowsT[:, g.slot(4), :], start=True, stop=False)
                                pe.matmul(h[:, :], w2a[:, 1, m * P:(m + 1) * P], aggT[:, g.slot(2), :], start=False, stop=True).then_inc(s_h, 1)
                        g = s.back(1)
                        if g.real():
                            if g.follows(1):
                                pe.wait_ge(s_mT, g.back(1).done(1))
                            pe.wait_ge(s_me, g.done(1))
                            for t in range(U):
                                mm = pe.transpose(tiles(bank[3])[:, t, :], agg[:, g.slot(2), t, :], ident[:, :])
                            mm.then_inc(s_Tm, 1)
                        g = s.back(3)
                        if g.real():
                            pe.wait_ge(s_hr, g.done(2))
                            if g.follows(1):
                                pe.wait_ge(norm.s_v, g.back(1).done(1))
                            for t in range(U):
                                pe.matmul(tiles(bank[6])[:, t, :], hidT[:, g.slot(2), 0, t * P:(t + 1) * P], w2b[:, 0, :], start=True, stop=False)
                                mm = pe.matmul(tiles(bank[6])[:, t, :], hidT[:, g.slot(2), 1, t * P:(t + 1) * P], w2b[:, 1, :], start=False, stop=True)
                            mm.then_inc(s_o, 1)
                        g = s
                        if g.real():
                            pe.wait_ge(s_oh, g.done(1))
                            if g.follows(1):
                                pe.wait_ge(s_me, g.back(1).done(1))
                            for t in range(U):
                                mm = pe.matmul(tiles(bank[1])[:, t, :], onehot[:, g.slot(2), t, :], window[:, g.slot(2), t, 0:D],
                                               start=True, stop=True)
                            mm.then_inc(s_ag, 1)
                    run_steps(pe, NODE_GROUPS, 3, step)

                @block.scalar
                def _(act):
                    def step(s):
                        if s.real():
                            g = s
                            if g.follows(4):
                                act.wait_ge(s_h, g.back(4).done(2))
                            act.wait_ge(s_T, g.done(1))
                            act.activation(rowsT[:, g.slot(4), :], bank[0][:, :], ACT.Copy).then_inc(s_xT, 1)
                        g = s.back(2)
                        if g.real():
                            if g.follows(2):
                                act.wait_ge(s_o, g.back(2).done(1))
                            for m in range(2):
                                act.wait_ge(s_h, g.number * 2 + (m + 1))
                                act.activation(hidT[:, g.slot(2), m, :], bank[4 + m][:, :], ACT.Relu, bias=c2_col[:, m:m + 1]).then_inc(s_hr, 1)
                        g = s.back(1)
                        if g.real():
                            if g.follows(2):
                                act.wait_ge(s_h, g.back(2).done(2))
                            act.wait_ge(s_Tm, g.done(1))
                            act.activation(aggT[:, g.slot(2), :], bank[3][:, :], ACT.Copy).then_inc(s_mT, 1)
                        g = s.back(3)
                        if g.real():
                            norm.deviation(act, g)
                        g = s.back(4)
                        if g.real():
                            norm.apply(act, g, s_put)
                    run_steps(act, NODE_GROUPS, 4, step)

                @block.vector
                def _(dve):
                    def step(s):
                        if s.real():
                            make_onehot(dve, s, s_oh, s_ag, s_win)
                        g = s.back(1)
                        if g.real():
                            if g.follows(2):
                                dve.wait_ge(s_Tm, g.back(2).done(1))
                            dve.wait_ge(s_ag, g.done(1))
                            for t in range(U):
                                d = dve.tensor_scalar(agg[:, g.slot(2), t, :], tiles(bank[1])[:, t, :],
                                                      inv_count[:, bass.ds(g.number * U + t, 1)], None, ALU.mult)
                            d.then_inc(s_me, 1)
                        g = s.back(4)
                        if g.real():
                            norm.scales(dve, g)
                        g = s.back(3)
                        if g.real():
                            if g.follows(2):
                                dve.wait_ge(norm.s_y, g.back(2).done(1))
                            dve.wait_ge(s_xb, g.done(1))
                            dve.wait_ge(s_o, g.done(1))
                            dve.tensor_tensor(val[:, g.slot(2), :, :], tiles(bank[6]), res[:, g.slot(4), :, :], ALU.add).then_inc(norm.s_v, 1)
                            norm.moments(dve, g)
                    run_steps(dve, NODE_GROUPS, 4, step)

        edge_conv("conv1", x, w1, messages[0], True)
        node_first("nodes1", messages[0])
        edge_conv("conv2", x1_tab, w2, messages[1], False)
        node_second("nodes2", messages[1])
        edge_mlp("mlp1", y_tab, messages[2])
        node_third("nodes3", messages[2])


_INS = ['x', 'src', 'dst', 'edge_attr_128', 'edge_weight1', 'L0_gnn_W1', 'L0_gnn_root1', 'L0_gnn_b1',
        'L0_gnn_W2', 'L0_gnn_root2', 'L0_gnn_b2', 'L1_gnn_u', 'L1_gnn_W1a', 'L1_gnn_b1a', 'L1_gnn_W1b',
        'L1_gnn_b1b', 'L1_gnn_W2a', 'L1_gnn_b2a', 'L1_gnn_W2b', 'L1_gnn_b2b']


def kernel(**inputs):
    import numpy as _np
    import concourse.bacc as _bacc
    from concourse.bass_utils import run_bass_kernel_spmd as _run

    nc = _bacc.Bacc("TRN2", target_bir_lowering=False, num_devices=1)
    arrays, args = {}, []
    for name in _INS:
        a = _np.ascontiguousarray(inputs[name])
        if name == 'edge_weight1':
            a = a.reshape(-1)
        arrays[f"in_{name}_dram"] = a
        args.append(nc.dram_tensor(f"in_{name}_dram", a.shape, mybir.dt.from_np(a.dtype), kind="ExternalInput").ap())
    out = nc.dram_tensor("out_0_dram", (arrays["in_x_dram"].shape[0], D), F32, kind="ExternalOutput").ap()
    build(nc, *args, out)
    r = _run(nc, [arrays], core_ids=[0])
    return r.results[0]["out_0_dram"]
```

```python
from contextlib import ExitStack

import concourse.bass as bass
from concourse import mybir
from concourse.bass import IndirectOffsetOnAxis

ALU = mybir.AluOpType
ACT = mybir.ActivationFunctionType
F32 = mybir.dt.float32
BF16 = mybir.dt.bfloat16
I32 = mybir.dt.int32

P = 128
U = 4
GROUP = P * U
D = 128
H = 256
COUNT = D
DEST = D + 1
ROW = D + 2
EPS = 1e-5
UNROLL = 4
LEAD = 8
NO_NODE = -1.0


class Group:

    def __init__(self, i, c, count):
        self.i, self.c, self.count = i, c, count
        self.static = isinstance(i, int)

    @property
    def number(self):
        return self.i * UNROLL + self.c

    def real(self):
        return not self.static or 0 <= self.number < self.count

    def back(self, n):
        return Group(self.i, self.c - n, self.count)

    def slot(self, slots):
        return self.c % slots

    def turn(self, slots):
        return self.i * (UNROLL // slots) + self.c // slots

    def follows(self, n):
        return not self.static or self.number >= n

    def done(self, per_group):
        return self.number * per_group + per_group

    def landed(self, per_group, slots):
        return self.turn(slots) * per_group + per_group

    def base(self, rows):
        if self.static:
            return min(GROUP * self.number, rows - GROUP)
        return self.i * (UNROLL * GROUP) + GROUP * self.c


def run_steps(eng, count, depth, step, ahead=0):
    turns = (count - 1 - ahead - LEAD) // UNROLL
    for c in range(LEAD):
        step(Group(0, c, count))
    first = LEAD // UNROLL
    with eng.Fori(first, first + turns) as i:
        for c in range(UNROLL):
            step(Group(i, c, count))
    for c in range(LEAD + turns * UNROLL, count + depth):
        step(Group(0, c, count))



def build(nc, x, src, dst, edge_attr, edge_weight, W1, root1, b1, W2, root2, b2,
          u_glob, W1a, b1a, W1b, b1b, W2a, b2a, W2b, b2b, out):
    N, E = x.shape[0], src.shape[0]
    NODE_GROUPS = -(-N // GROUP)
    EDGE_GROUPS = -(-E // GROUP)
    NT = NODE_GROUPS * U
    FIRST_LAST = N - GROUP
    NEW_IN_LAST = GROUP * (EDGE_GROUPS - 1) - (E - GROUP)
    assert NEW_IN_LAST % U == 0

    ctx = ExitStack()
    with ctx:
        def sb(name, shape, dt=F32):
            return ctx.enter_context(nc.sbuf_tensor(name, shape, dt))

        def pb(name, shape, dt=F32):
            return ctx.enter_context(nc.psum_tensor(name, shape, dt))

        held = {"now": [], "before": []}

        def sem(name):
            held["now"].append(nc.alloc_semaphore(name=name))
            return held["now"][-1]

        def free_finished_phase():
            if held["before"]:
                nc.clear_and_free_semaphores(held["before"])
            held["before"], held["now"] = held["now"], []

        def sems(name, n):
            return [sem(f"{name}{k}") for k in range(n)]

        x1_tab = nc.dram_tensor("x1_tab", (N, D), F32).ap()
        z_tab = nc.dram_tensor("z_tab", (N, D), F32).ap()
        y_tab = nc.dram_tensor("y_tab", (N, D), F32).ap()
        messages = [nc.dram_tensor(f"messages{k}", (E + P, ROW), F32).ap() for k in range(3)]

        ident = sb("ident", [P, P])
        node_iota = sb("node_iota", [P, P])
        starts = sb("starts", [P, NT])
        count_w = sb("count_w", [P, 2], BF16)
        start_row = sb("start_row", [1, -(-NT // (U * UNROLL)) * U * UNROLL], I32)
        inv_count = sb("inv_count", [P, NT])
        pad_rows = sb("pad_rows", [P, ROW])
        eps = sb("eps", [P, 1])
        w1 = sb("w1", [P, 2, D])
        w2 = sb("w2", [P, 2, D])
        r1 = sb("r1", [P, D])
        r2 = sb("r2", [P, D])
        w1a = sb("w1a", [P, 2, H])
        w1b = sb("w1b", [P, 2, D])
        w2a = sb("w2a", [P, 3, H])
        w2b = sb("w2b", [P, 2, D])
        b1_bc = sb("b1_bc", [P, D])
        b2_bc = sb("b2_bc", [P, D])
        b1b_bc = sb("b1b_bc", [P, D])
        b2b_bc = sb("b2b_bc", [P, D])
        b1a_col = sb("b1a_col", [P, 2])
        b2a_col = sb("b2a_col", [P, 2])
        c2_col = sb("c2_col", [P, 2])
        u_col = sb("u_col", [P, 1])

        src_t = sb("src_t", [P, 4, U], I32)
        dst_t = sb("dst_t", [P, 4, U], I32)
        u_t = sb("u_t", [P, 4, U])
        omu = sb("omu", [P, 2, U])
        below = sb("below", [P, 2, U, NT], BF16)
        rows = sb("rows", [P, 4, U, D])
        rowsT = sb("rowsT", [P, 4, GROUP])
        attr = sb("attr", [P, 2, U, D])
        attrT = sb("attrT", [P, 2, GROUP])
        hidT = sb("hidT", [P, 2, 2, GROUP])
        part0 = sb("part0", [P, 2, U, D])
        mess = sb("mess", [P, 4, U, ROW])
        window = sb("window", [P, 4, U, ROW])
        dest_rel = sb("dest_rel", [P, 4, U])
        onehot = sb("onehot", [P, 2, U, P])
        agg = sb("agg", [P, 2, U, D])
        aggT = sb("aggT", [P, 2, GROUP])
        cnt = sb("cnt", [P, 2, U])
        res = sb("res", [P, 4, U, D])
        val = sb("val", [P, 4, U, D])
        stats = sb("stats", [P, 4, U, 6])
        mv = sb("mv", [P, 4, U, 2])
        std = sb("std", [P, 4, U])
        rstd = sb("rstd", [P, 4, U])
        nmr = sb("nmr", [P, 4, U])
        done = sb("done", [P, 2, U, D])

        bank = [pb(f"bank{k}", [P, GROUP]) for k in range(8)]

        def tiles(b):
            return b[:, :].rearrange("p (u f) -> p u f", u=U)

        s_w = sem("weights_loaded")
        s_pad = sem("pad_made")
        s_padst = sem("pad_stored")
        s_c0 = sem("const_filled")
        s_c1 = sem("const_ready")
        s_c2 = sem("glob_product")
        s_c2d = sem("glob_added")
        free_finished_phase()
        with nc.Block() as block:
            @block.sync
            def _(sp):
                for t, w in ((w1[:, :, :], W1.rearrange("k d o -> d k o")), (w2[:, :, :], W2.rearrange("k d o -> d k o")),
                             (r1[:, :], root1), (r2[:, :], root2),
                             (w1a[:, :, :], W1a.rearrange("(k p) n -> p k n", p=P)),
                             (w1b[:, :, :], W1b.rearrange("(k p) n -> p k n", p=P)),
                             (w2a[:, :, :], W2a.rearrange("(k p) n -> p k n", p=P)),
                             (w2b[:, :, :], W2b.rearrange("(k p) n -> p k n", p=P)),
                             (b1_bc[:, :], b1.partition_broadcast(P)), (b2_bc[:, :], b2.partition_broadcast(P)),
                             (b1b_bc[:, :], b1b.partition_broadcast(P)), (b2b_bc[:, :], b2b.partition_broadcast(P))):
                    sp.dma_start(t, w).then_inc(s_w, 16)
                sp.dma_start(b1a_col[:, :], b1a.rearrange("(m p) -> p m", p=P), allow_slow_non_contiguous=True).then_inc(s_w, 16)
                sp.dma_start(b2a_col[:, :], b2a.rearrange("(m p) -> p m", p=P), allow_slow_non_contiguous=True).then_inc(s_w, 16)
                sp.dma_start(u_col[:, :], u_glob[0:1, :].rearrange("a p -> p a"), allow_slow_non_contiguous=True).then_inc(s_w, 16)
                sp.wait_ge(s_pad, 2)
                for m in messages:
                    sp.dma_start(m[E:E + P, :], pad_rows[:, :]).then_inc(s_padst, 16)
                sp.wait_ge(s_padst, 16 * len(messages))
                sp.wait_ge(s_w, 16 * 15)

            @block.gpsimd
            def _(pool):
                pool.memset(ident[:, :], 0.0).then_inc(s_c0, 1)
                pool.memset(count_w[:, :], 1.0).then_inc(s_c0, 1)
                pool.iota(node_iota[:, :], [[1, P]], base=0, channel_multiplier=0, allow_small_or_imprecise_dtypes=True)
                pool.iota(starts[:, 0:NT - U], [[P, NT - U]], base=0, channel_multiplier=0, allow_small_or_imprecise_dtypes=True)
                pool.iota(starts[:, NT - U:NT], [[P, U]], base=FIRST_LAST, channel_multiplier=0, allow_small_or_imprecise_dtypes=True)
                pool.wait_ge(s_c0, 2)
                pool.affine_select(out=ident[:, :], in_=ident[:, :], compare_op=ALU.not_equal, fill=1.0,
                                   base=0, pattern=[[-1, P]], channel_multiplier=1)
                pool.affine_select(out=count_w[:, 1:2], in_=count_w[:, 1:2], compare_op=ALU.is_ge, fill=0.0,
                                   base=-(NEW_IN_LAST // U), pattern=[[0, 1]], channel_multiplier=1).then_inc(s_c1, 1)

            @block.tensor
            def _(pe):
                pe.wait_ge(s_w, 16 * 15)
                for m in range(2):
                    mm = pe.matmul(bank[0][:, m:m + 1], w2a[:, 2, m * P:(m + 1) * P], u_col[:, :], start=True, stop=True)
                mm.then_inc(s_c2, 1)

            @block.vector
            def _(dve):
                dve.memset(pad_rows[:, 0:DEST], 0.0).then_inc(s_pad, 1)
                dve.memset(pad_rows[:, DEST:ROW], NO_NODE).then_inc(s_pad, 1)
                dve.memset(mess[:, :, :, COUNT:COUNT + 1], 1.0)
                dve.memset(eps[:, :], EPS)
                dve.memset(start_row[:, :], 0)
                dve.wait_ge(s_c2, 1)
                dve.tensor_tensor(c2_col[:, :], bank[0][:, 0:2], b2a_col[:, :], ALU.add).then_inc(s_c2d, 1)

        def edge_values(v, at):
            return v[bass.ds(at, GROUP)].rearrange("(p u) -> p u", u=U)

        def edge_conv(name, table, w, out_rows, counting):
            s_src = sems(name + "_sources_loaded", 4)
            s_idx = sems(name + "_edges_loaded", 4)
            s_got = sems(name + "_rows_gathered", 4)
            s_go = sem(name + "_gather_released")
            s_free = sem(name + "_edge_slot_released")
            s_put = sems(name + "_messages_stored", 4)
            s_T = sem(name + "_rows_transposed")
            s_xT = sem(name + "_rowsT_copied")
            s_mm = sem(name + "_products")
            s_om = sem(name + "_omu_ready")
            s_df = sem(name + "_dest_ready")
            s_t0 = sem(name + "_part0_ready")
            s_ms = sem(name + "_messages_ready")
            s_bl = sem(name + "_below_ready")
            s_ct = sem(name + "_below_summed")
            free_finished_phase()
            with nc.Block() as block:
                @block.sync
                def _(sp):
                    def load_sources(g):
                        if g.real():
                            if g.follows(4):
                                sp.wait_ge(s_T, g.back(4).done(1))
                            at = sp.snap(g.base(E)) if not g.static else g.base(E)
                            sp.dma_start(src_t[:, g.slot(4), :], edge_values(src, at)).then_inc(s_src[g.slot(4)], 16)

                    def step(s):
                        load_sources(s.back(-2))
                        if s.real():
                            g = s
                            if g.follows(4):
                                sp.wait_ge(s_ms, g.back(4).done(1))
                                sp.sem_inc(s_free, 1)
                            at = sp.snap(g.base(E)) if not g.static else g.base(E)
                            for t, v in ((dst_t, dst), (u_t, edge_weight)):
                                sp.dma_start(t[:, g.slot(4), :], edge_values(v, at)).then_inc(s_idx[g.slot(4)], 16)
                        g = s.back(3)
                        if g.real():
                            at = sp.snap(g.base(E)) if not g.static else g.base(E)
                            sp.wait_ge(s_ms, g.done(1))
                            if g.static and g.number == EDGE_GROUPS - 1:
                                if g.follows(1):
                                    sp.wait_ge(s_put[g.back(1).slot(4)], g.back(1).landed(16, 4))
                            sp.dma_start(out_rows[bass.ds(at, GROUP), :].rearrange("(p u) f -> p u f", u=U),
                                         mess[:, g.slot(4), :, :]).then_inc(s_put[g.slot(4)], 16)
                    for n in range(2):
                        load_sources(Group(0, n, EDGE_GROUPS))
                    run_steps(sp, EDGE_GROUPS, 3, step, ahead=2)
                    for n in range(EDGE_GROUPS - 4, EDGE_GROUPS):
                        g = Group(0, n, EDGE_GROUPS)
                        sp.wait_ge(s_put[g.slot(4)], g.landed(16, 4))

                @block.gpsimd
                def _(pool):
                    top = pool.to_reg(N - 1)

                    def step(g):
                        if g.real():
                            pool.wait_ge(s_src[g.slot(4)], g.landed(16, 4))
                            if g.follows(4):
                                pool.wait_ge(s_T, g.back(4).done(1))
                            pool.sem_inc(s_go, 1)
                            for t in range(U):
                                pool.indirect_dma_start(rows[:, g.slot(4), t, :], None, table,
                                                        IndirectOffsetOnAxis(ap=src_t[:, g.slot(4), t:t + 1], axis=0),
                                                        bounds_check=top, oob_is_err=False).then_inc(s_got[g.slot(4)], 16)
                    run_steps(pool, EDGE_GROUPS, 0, step)

                @block.tensor
                def _(pe):
                    def step(s):
                        if s.real():
                            g = s
                            if g.follows(1):
                                pe.wait_ge(s_xT, g.back(1).done(1))
                            pe.wait_ge(s_got[g.slot(4)], g.landed(16 * U, 4))
                            for t in range(U):
                                mm = pe.transpose(tiles(bank[0])[:, t, :], rows[:, g.slot(4), t, :], ident[:, :])
                            mm.then_inc(s_T, 1)
                        g = s.back(1)
                        if g.real():
                            pe.wait_ge(s_xT, g.done(1))
                            if g.follows(2):
                                pe.wait_ge(s_ms, g.back(2).done(1))
                            for t in range(U):
                                b = bank[1 + 2 * g.slot(2) + t // 2]
                                mm = pe.matmul(b[:, (t % 2) * 2 * D:(t % 2 + 1) * 2 * D], rowsT[:, g.slot(2), t * P:(t + 1) * P],
                                               w[:, :, :].rearrange("p k o -> p (k o)"), start=True, stop=True)
                            mm.then_inc(s_mm, 1)
                            if counting:
                                pe.wait_ge(s_bl, g.done(1))
                                last = g.static and g.number == EDGE_GROUPS - 1
                                for t in range(U):
                                    mm = pe.matmul(bank[5][0:1, 0:NT], count_w[:, int(last):int(last) + 1], below[:, g.slot(2), t, :],
                                                   start=(g.static and g.number == 0 and t == 0), stop=(last and t == U - 1))
                                mm.then_inc(s_ct, 1)
                    run_steps(pe, EDGE_GROUPS, 1, step)

                @block.scalar
                def _(act):
                    def step(s):
                        if s.real():
                            g = s
                            if g.follows(2):
                                act.wait_ge(s_mm, g.back(2).done(1))
                            act.wait_ge(s_T, g.done(1))
                            act.activation(rowsT[:, g.slot(2), :], bank[0][:, :], ACT.Copy).then_inc(s_xT, 1)
                        g = s.back(1)
                        if g.real():
                            act.wait_ge(s_om, g.done(1))
                            if g.follows(2):
                                act.wait_ge(s_ms, g.back(2).done(1))
                            act.wait_ge(s_mm, g.done(1))
                            for t in range(U):
                                b = bank[1 + 2 * g.slot(2) + t // 2]
                                a = act.activation(part0[:, g.slot(2), t, :], b[:, (t % 2) * 2 * D:(t % 2) * 2 * D + D], ACT.Copy,
                                                   scale=omu[:, g.slot(2), t:t + 1])
                            a.then_inc(s_t0, 1)
                    run_steps(act, EDGE_GROUPS, 1, step)

                @block.vector
                def _(dve):
                    def step(s):
                        if s.real():
                            g = s
                            if g.follows(2):
                                dve.wait_ge(s_t0, g.back(2).done(1))
                            dve.wait_ge(s_idx[g.slot(4)], g.landed(32, 4))
                            dve.tensor_scalar(omu[:, g.slot(2), :], u_t[:, g.slot(4), :], -1.0, 1.0, ALU.mult, ALU.add).then_inc(s_om, 1)
                            if g.follows(4):
                                dve.wait_ge(s_put[g.slot(4)], g.back(4).landed(16, 4))
                            dve.tensor_copy(mess[:, g.slot(4), :, DEST:ROW].rearrange("p u a -> p (u a)"), dst_t[:, g.slot(4), :]).then_inc(s_df, 1)
                            if counting:
                                if g.follows(2):
                                    dve.wait_ge(s_ct, g.back(2).done(1))
                                dve.wait_ge(s_df, g.done(1))
                                for t in range(U):
                                    d = dve.tensor_scalar(below[:, g.slot(2), t, :], starts[:, :], mess[:, g.slot(4), t, DEST:ROW],
                                                          None, ALU.is_gt)
                                d.then_inc(s_bl, 1)
                        g = s.back(1)
                        if g.real():
                            dve.wait_ge(s_t0, g.done(1))
                            for t in range(U):
                                b = bank[1 + 2 * g.slot(2) + t // 2]
                                d = dve.scalar_tensor_tensor(out=mess[:, g.slot(4), t, 0:D], in0=b[:, (t % 2) * 2 * D + D:(t % 2 + 1) * 2 * D],
                                                             scalar=u_t[:, g.slot(4), t:t + 1], in1=part0[:, g.slot(2), t, :],
                                                             op0=ALU.mult, op1=ALU.add)
                            d.then_inc(s_ms, 1)
                    run_steps(dve, EDGE_GROUPS, 1, step)
                    if counting:
                        dve.wait_ge(s_ct, EDGE_GROUPS)
                        dve.tensor_copy(start_row[:, 0:NT], bank[5][0:1, 0:NT])

        def edge_mlp(name, table, out_rows):
            s_src = sems(name + "_sources_loaded", 4)
            s_idx = sems(name + "_edges_loaded", 4)
            s_at = sems(name + "_attributes_loaded", 2)
            s_got = sems(name + "_rows_gathered", 4)
            s_go = sem(name + "_gather_released")
            s_free = sem(name + "_edge_slot_released")
            s_put = sems(name + "_messages_stored", 4)
            s_T = sem(name + "_rows_transposed")
            s_aT = sem(name + "_attributes_transposed")
            s_xTc = sem(name + "_rowsT_copied")
            s_aTc = sem(name + "_attrT_copied")
            s_h = sem(name + "_hidden_products")
            s_hr = sem(name + "_hidden_ready")
            s_o = sem(name + "_outputs_products")
            s_df = sem(name + "_dest_ready")
            s_ms = sem(name + "_messages_ready")
            free_finished_phase()
            with nc.Block() as block:
                @block.sync
                def _(sp):
                    def load_sources(g):
                        if g.real():
                            if g.follows(4):
                                sp.wait_ge(s_T, g.back(4).done(1))
                            at = sp.snap(g.base(E)) if not g.static else g.base(E)
                            sp.dma_start(src_t[:, g.slot(4), :], edge_values(src, at)).then_inc(s_src[g.slot(4)], 16)

                    def step(s):
                        load_sources(s.back(-2))
                        if s.real():
                            g = s
                            if g.follows(4):
                                sp.wait_ge(s_ms, g.back(4).done(1))
                                sp.sem_inc(s_free, 1)
                            at = sp.snap(g.base(E)) if not g.static else g.base(E)
                            if g.follows(2):
                                sp.wait_ge(s_aT, g.back(2).done(1))
                            sp.dma_start(attr[:, g.slot(2), :, :],
                                         edge_attr[bass.ds(at, GROUP), :].rearrange("(p u) f -> p u f", u=U)).then_inc(s_at[g.slot(2)], 16)
                            sp.dma_start(dst_t[:, g.slot(4), :], edge_values(dst, at)).then_inc(s_idx[g.slot(4)], 16)
                        g = s.back(4)
                        if g.real():
                            at = sp.snap(g.base(E)) if not g.static else g.base(E)
                            sp.wait_ge(s_ms, g.done(1))
                            if g.static and g.number == EDGE_GROUPS - 1:
                                if g.follows(1):
                                    sp.wait_ge(s_put[g.back(1).slot(4)], g.back(1).landed(16, 4))
                            sp.dma_start(out_rows[bass.ds(at, GROUP), :].rearrange("(p u) f -> p u f", u=U),
                                         mess[:, g.slot(4), :, :]).then_inc(s_put[g.slot(4)], 16)
                    for n in range(2):
                        load_sources(Group(0, n, EDGE_GROUPS))
                    run_steps(sp, EDGE_GROUPS, 4, step, ahead=2)
                    for n in range(EDGE_GROUPS - 4, EDGE_GROUPS):
                        g = Group(0, n, EDGE_GROUPS)
                        sp.wait_ge(s_put[g.slot(4)], g.landed(16, 4))

                @block.gpsimd
                def _(pool):
                    top = pool.to_reg(N - 1)

                    def step(g):
                        if g.real():
                            pool.wait_ge(s_src[g.slot(4)], g.landed(16, 4))
                            if g.follows(4):
                                pool.wait_ge(s_T, g.back(4).done(1))
                            pool.sem_inc(s_go, 1)
                            for t in range(U):
                                pool.indirect_dma_start(rows[:, g.slot(4), t, :], None, table,
                                                        IndirectOffsetOnAxis(ap=src_t[:, g.slot(4), t:t + 1], axis=0),
                                                        bounds_check=top, oob_is_err=False).then_inc(s_got[g.slot(4)], 16)
                    run_steps(pool, EDGE_GROUPS, 0, step)

                @block.tensor
                def _(pe):
                    def step(s):
                        if s.real():
                            g = s
                            if g.follows(1):
                                pe.wait_ge(s_aTc, g.back(1).done(1))
                            pe.wait_ge(s_at[g.slot(2)], g.landed(16, 2))
                            for t in range(U):
                                mm = pe.transpose(tiles(bank[1])[:, t, :], attr[:, g.slot(2), t, :], ident[:, :])
                            mm.then_inc(s_aT, 1)
                            if g.follows(1):
                                pe.wait_ge(s_xTc, g.back(1).done(1))
                            pe.wait_ge(s_got[g.slot(4)], g.landed(16 * U, 4))
                            for t in range(U):
                                mm = pe.transpose(tiles(bank[0])[:, t, :], rows[:, g.slot(4), t, :], ident[:, :])
                            mm.then_inc(s_T, 1)
                        g = s.back(1)
                        if g.real():
                            pe.wait_ge(s_aTc, g.done(1))
                            pe.wait_ge(s_xTc, g.done(1))
                            if g.follows(1):
                                pe.wait_ge(s_hr, g.back(1).done(2))
                            for m in range(2):
                                h = bank[2 + m]
                                pe.matmul(h[:, :], w1a[:, 1, m * P:(m + 1) * P], attrT[:, g.slot(2), :], start=True, stop=False)
                                pe.matmul(h[:, :], w1a[:, 0, m * P:(m + 1) * P], rowsT[:, g.slot(2), :], start=False, stop=True).then_inc(s_h, 1)
                        g = s.back(2)
                        if g.real():
                            pe.wait_ge(s_hr, g.done(2))
                            if g.follows(1):
                                pe.wait_ge(s_ms, g.back(1).done(1))
                            for t in range(U):
                                pe.matmul(tiles(bank[4])[:, t, :], hidT[:, g.slot(2), 0, t * P:(t + 1) * P], w1b[:, 0, :], start=True, stop=False)
                                mm = pe.matmul(tiles(bank[4])[:, t, :], hidT[:, g.slot(2), 1, t * P:(t + 1) * P], w1b[:, 1, :], start=False, stop=True)
                            mm.then_inc(s_o, 1)
                    run_steps(pe, EDGE_GROUPS, 2, step)

                @block.scalar
                def _(act):
                    def step(s):
                        if s.real():
                            g = s
                            if g.follows(2):
                                act.wait_ge(s_h, g.back(2).done(2))
                            act.wait_ge(s_T, g.done(1))
                            act.activation(rowsT[:, g.slot(2), :], bank[0][:, :], ACT.Copy).then_inc(s_xTc, 1)
                        g = s.back(1)
                        if g.real():
                            if g.follows(2):
                                act.wait_ge(s_o, g.back(2).done(1))
                            for m in range(2):
                                act.wait_ge(s_h, g.number * 2 + (m + 1))
                                act.activation(hidT[:, g.slot(2), m, :], bank[2 + m][:, :], ACT.Relu, bias=b1a_col[:, m:m + 1]).then_inc(s_hr, 1)
                    run_steps(act, EDGE_GROUPS, 1, step)

                @block.vector
                def _(dve):
                    def step(s):
                        if s.real():
                            g = s
                            if g.follows(2):
                                dve.wait_ge(s_h, g.back(2).done(2))
                            dve.wait_ge(s_aT, g.done(1))
                            dve.tensor_copy(attrT[:, g.slot(2), :], bank[1][:, :]).then_inc(s_aTc, 1)
                        g = s.back(2)
                        if g.real():
                            dve.wait_ge(s_idx[g.slot(4)], g.landed(16, 4))
                            if g.follows(4):
                                dve.wait_ge(s_put[g.slot(4)], g.back(4).landed(16, 4))
                            dve.tensor_copy(mess[:, g.slot(4), :, DEST:ROW].rearrange("p u a -> p (u a)"), dst_t[:, g.slot(4), :])
                            dve.wait_ge(s_o, g.done(1))
                            for t in range(U):
                                d = dve.tensor_tensor(mess[:, g.slot(4), t, 0:D], tiles(bank[4])[:, t, :], b1b_bc[:, :], ALU.add)
                            d.then_inc(s_ms, 1)
                    run_steps(dve, EDGE_GROUPS, 2, step)

        def load_windows(sp, g, table, s_win, regs):
            if g.c % UNROLL == 0:
                sp.load(regs, start_row[0:1, bass.ds(g.number * U, U * UNROLL)])
            for t in range(U):
                at = sp.snap(regs[(g.c % UNROLL) * U + t], min_val=0, max_val=E)
                sp.dma_start(window[:, g.slot(4), t, :], table[bass.ds(at, P), :]).then_inc(s_win[g.slot(4)], 16)

        def relative_dest(pool, g, s_win, s_oh, s_dr):
            if g.follows(4):
                pool.wait_ge(s_oh, g.back(4).done(1))
            pool.wait_ge(s_win[g.slot(4)], g.landed(16 * U, 4))
            pool.tensor_tensor(dest_rel[:, g.slot(4), :], window[:, g.slot(4), :, DEST], starts[:, bass.ds(g.number * U, U)],
                               ALU.subtract).then_inc(s_dr, 1)

        def make_onehot(dve, g, s_oh, s_ag, s_dr):
            if g.follows(2):
                dve.wait_ge(s_ag, g.back(2).done(1))
            dve.wait_ge(s_dr, g.done(1))
            dve.tensor_tensor(onehot[:, g.slot(2), :, :], node_iota[:, :].unsqueeze(1).to_broadcast([P, U, P]),
                              dest_rel[:, g.slot(4), :].unsqueeze(2).to_broadcast([P, U, P]), ALU.is_equal).then_inc(s_oh, 1)

        def node_rows(table, at):
            return table[bass.ds(at, GROUP), :].rearrange("(u p) f -> p u f", p=P)

        def node_first(name, table):
            s_x = sems(name + "_x_loaded", 4)
            s_win = sems(name + "_windows_loaded", 4)
            s_dr = sem(name + "_dest_relative")
            s_px1 = sems(name + "_x1_stored", 4)
            s_pz = sems(name + "_z_stored", 2)
            s_T = sem(name + "_x_transposed")
            s_xT = sem(name + "_xT_copied")
            s_oh = sem(name + "_onehot_ready")
            s_ag = sem(name + "_sums")
            s_r1 = sem(name + "_root1_product")
            s_ct = sem(name + "_count_read")
            s_iv = sem(name + "_inverse_ready")
            s_me = sem(name + "_mean_ready")
            s_x1 = sem(name + "_x1_ready")
            s_T1 = sem(name + "_x1_transposed")
            s_x1T = sem(name + "_x1T_copied")
            s_r2 = sem(name + "_root2_product")
            s_xb = sem(name + "_x_plus_bias")
            s_z = sem(name + "_z_ready")
            s_mb = sem(name + "_biased_mean_ready")
            r1_bank = (1, 6)
            x1 = val
            z = done
            x1T = aggT
            free_finished_phase()
            with nc.Block() as block:
                @block.sync
                def _(sp):
                    regs = [ctx.enter_context(sp.register(name=f"{name}_start{t}")) for t in range(U * UNROLL)]

                    def step(s):
                        if s.real():
                            g = s
                            at = sp.snap(g.base(N)) if not g.static else g.base(N)
                            if g.follows(4):
                                sp.wait_ge(s_T, g.back(4).done(1))
                            if g.follows(4):
                                sp.wait_ge(s_xb, g.back(4).done(1))
                            sp.dma_start(rows[:, g.slot(4), :, :], node_rows(x, at)).then_inc(s_x[g.slot(4)], 16)
                            if g.follows(4):
                                sp.wait_ge(s_ag, g.back(4).done(1))
                            load_windows(sp, g, table, s_win, regs)
                    run_steps(sp, NODE_GROUPS, 0, step)

                @block.gpsimd
                def _(pool):
                    def step(s):
                        if s.real():
                            relative_dest(pool, s, s_win, s_oh, s_dr)
                        g = s.back(1)
                        if g.real():
                            if g.follows(4):
                                pool.wait_ge(s_z, g.back(4).done(1))
                            pool.wait_ge(s_x[g.slot(4)], g.landed(16, 4))
                            for t in range(U):
                                p = pool.tensor_tensor(res[:, g.slot(4), t, :], rows[:, g.slot(4), t, :], b2_bc[:, :], ALU.add)
                            p.then_inc(s_xb, 1)
                    run_steps(pool, NODE_GROUPS, 1, step)

                @block.tensor
                def _(pe):
                    def step(s):
                        g = s
                        if g.real():
                            if g.follows(1):
                                pe.wait_ge(s_xT, g.back(1).done(1))
                            pe.wait_ge(s_x[g.slot(4)], g.landed(16, 4))
                            for t in range(U):
                                mm = pe.transpose(tiles(bank[0])[:, t, :], rows[:, g.slot(4), t, :], ident[:, :])
                            mm.then_inc(s_T, 1)
                        g = s.back(1)
                        if g.real():
                            pe.wait_ge(s_xT, g.done(1))
                            if g.follows(2):
                                pe.wait_ge(s_x1, g.back(2).done(1))
                            for t in range(U):
                                mm = pe.matmul(tiles(bank[r1_bank[g.slot(2)]])[:, t, :], rowsT[:, g.slot(2), t * P:(t + 1) * P], r1[:, :],
                                               start=True, stop=True)
                            mm.then_inc(s_r1, 1)
                        g = s.back(4)
                        if g.real():
                            pe.wait_ge(s_x1T, g.done(1))
                            if g.follows(1):
                                pe.wait_ge(s_z, g.back(1).done(1))
                            for t in range(U):
                                mm = pe.matmul(tiles(bank[5])[:, t, :], x1T[:, g.slot(2), t * P:(t + 1) * P], r2[:, :], start=True, stop=True)
                            mm.then_inc(s_r2, 1)
                        g = s.back(3)
                        if g.real():
                            if g.follows(1):
                                pe.wait_ge(s_x1T, g.back(1).done(1))
                            pe.wait_ge(s_x1, g.done(1))
                            for t in range(U):
                                mm = pe.transpose(tiles(bank[4])[:, t, :], x1[:, g.slot(4), t, :], ident[:, :])
                            mm.then_inc(s_T1, 1)
                        g = s
                        if g.real():
                            pe.wait_ge(s_oh, g.done(1))
                            if g.follows(1):
                                pe.wait_ge(s_me, g.back(1).done(1))
                            for t in range(U):
                                mm = pe.matmul(bank[2 + t // 2][:, (t % 2) * 256:(t % 2) * 256 + D + 1], onehot[:, g.slot(2), t, :],
                                               window[:, g.slot(4), t, 0:D + 1], start=True, stop=True)
                            mm.then_inc(s_ag, 1)
                    run_steps(pe, NODE_GROUPS, 4, step)

                @block.scalar
                def _(act):
                    def step(s):
                        g = s.back(1)
                        if g.real():
                            if g.follows(2):
                                act.wait_ge(s_mb, g.back(2).done(1))
                            act.wait_ge(s_iv, g.done(1))
                            for t in range(U):
                                a = act.activation(agg[:, g.slot(2), t, :], bank[2 + t // 2][:, (t % 2) * 256:(t % 2) * 256 + D], ACT.Copy,
                                                   scale=inv_count[:, bass.ds(g.number * U + t, 1)])
                            a.then_inc(s_me, 1)
                        g = s
                        if g.real():
                            if g.follows(2):
                                act.wait_ge(s_r1, g.back(2).done(1))
                            act.wait_ge(s_T, g.done(1))
                            act.activation(rowsT[:, g.slot(2), :], bank[0][:, :], ACT.Copy).then_inc(s_xT, 1)
                        g = s.back(3)
                        if g.real():
                            if g.follows(2):
                                act.wait_ge(s_r2, g.back(2).done(1))
                            act.wait_ge(s_T1, g.done(1))
                            act.activation(x1T[:, g.slot(2), :], bank[4][:, :], ACT.Copy).then_inc(s_x1T, 1)
                        g = s.back(3)
                        if g.real():
                            at = act.snap(g.base(N)) if not g.static else g.base(N)
                            act.wait_ge(s_x1, g.done(1))
                            if g.static and g.number == NODE_GROUPS - 1:
                                act.wait_ge(s_px1[g.back(1).slot(4)], g.back(1).landed(16, 4))
                            act.dma_start(node_rows(x1_tab, at), x1[:, g.slot(4), :, :]).then_inc(s_px1[g.slot(4)], 16)
                        g = s.back(5)
                        if g.real():
                            at = act.snap(g.base(N)) if not g.static else g.base(N)
                            act.wait_ge(s_z, g.done(1))
                            if g.static and g.number == NODE_GROUPS - 1:
                                act.wait_ge(s_pz[g.back(1).slot(2)], g.back(1).landed(16, 2))
                            act.dma_start(node_rows(z_tab, at), z[:, g.slot(2), :, :]).then_inc(s_pz[g.slot(2)], 16)
                    run_steps(act, NODE_GROUPS, 5, step)
                    for n in range(NODE_GROUPS - 4, NODE_GROUPS):
                        g = Group(0, n, NODE_GROUPS)
                        act.wait_ge(s_px1[g.slot(4)], g.landed(16, 4))
                    for n in range(NODE_GROUPS - 2, NODE_GROUPS):
                        g = Group(0, n, NODE_GROUPS)
                        act.wait_ge(s_pz[g.slot(2)], g.landed(16, 2))

                @block.vector
                def _(dve):
                    def step(s):
                        g = s.back(1)
                        if g.real():
                            dve.wait_ge(s_ag, g.done(1))
                            for b in range(2):
                                d = dve.tensor_scalar(cnt[:, g.slot(2), 2 * b:2 * b + 2], bank[2 + b][:, D::256], 1.0, None, ALU.max)
                            d.then_inc(s_ct, 1)
                            dve.wait_ge(s_ct, g.done(1))
                            dve.reciprocal(inv_count[:, bass.ds(g.number * U, U)], cnt[:, g.slot(2), :]).then_inc(s_iv, 1)
                        if s.real():
                            make_onehot(dve, s, s_oh, s_ag, s_dr)
                        g = s.back(4)
                        if g.real():
                            if g.follows(2):
                                dve.wait_ge(s_pz[g.slot(2)], g.back(2).landed(16, 2))
                            dve.wait_ge(s_xb, g.done(1))
                            dve.wait_ge(s_r2, g.done(1))
                            dve.tensor_tensor(z[:, g.slot(2), :, :], tiles(bank[5]), res[:, g.slot(4), :, :], ALU.add).then_inc(s_z, 1)
                        g = s.back(1)
                        if g.real():
                            if g.follows(2):
                                dve.wait_ge(s_x1, g.back(2).done(1))
                            dve.wait_ge(s_me, g.done(1))
                            dve.tensor_tensor(part0[:, g.slot(2), :, :], agg[:, g.slot(2), :, :],
                                              b1_bc[:, :].unsqueeze(1).to_broadcast([P, U, D]), ALU.add).then_inc(s_mb, 1)
                        g = s.back(2)
                        if g.real():
                            if g.follows(4):
                                dve.wait_ge(s_px1[g.slot(4)], g.back(4).landed(16, 4))
                                dve.wait_ge(s_T1, g.back(4).done(1))
                            dve.wait_ge(s_r1, g.done(1))
                            dve.wait_ge(s_mb, g.done(1))
                            dve.tensor_tensor(x1[:, g.slot(4), :, :], tiles(bank[r1_bank[g.slot(2)]]), part0[:, g.slot(2), :, :],
                                              ALU.add).then_inc(s_x1, 1)
                    run_steps(dve, NODE_GROUPS, 4, step)

        class Norm:

            def __init__(self, name):
                self.s_v = sem(name + "_value_ready")
                self.s_bs = sem(name + "_stats_ready")
                self.s_go = sem(name + "_aggregation_released")
                self.s_mv = sem(name + "_moments_ready")
                self.s_sd = sem(name + "_deviation_ready")
                self.s_rs = sem(name + "_rstd_ready")
                self.s_nm = sem(name + "_shift_ready")
                self.s_y = sem(name + "_normed")

            def moments(self, dve, g):
                k = g.slot(4)
                dve.wait_ge(self.s_v, g.done(1))
                for t in range(U):
                    d = dve.bn_stats(stats[:, k, t, :], val[:, k, t, :])
                d.then_inc(self.s_bs, 1)
                if g.follows(4):
                    dve.wait_ge(self.s_sd, g.back(4).done(1))
                dve.wait_ge(self.s_bs, g.done(1))
                dve.sem_inc(self.s_go, 1)
                for t in range(U):
                    d = dve.bn_aggr(mv[:, k, t, :], stats[:, k, t, :])
                d.then_inc(self.s_mv, 1)

            def deviation(self, act, g):
                k = g.slot(4)
                act.wait_ge(self.s_mv, g.done(1))
                if g.follows(4):
                    act.wait_ge(self.s_rs, g.back(4).done(1))
                act.activation(std[:, k, :], mv[:, k, :, 1], ACT.Sqrt, bias=eps[:, :]).then_inc(self.s_sd, 1)

            def scales(self, dve, g):
                k = g.slot(4)
                dve.wait_ge(self.s_sd, g.done(1))
                if g.follows(4):
                    dve.wait_ge(self.s_y, g.back(4).done(1))
                dve.reciprocal(rstd[:, k, :], std[:, k, :]).then_inc(self.s_rs, 1)
                dve.wait_ge(self.s_rs, g.done(1))
                dve.scalar_tensor_tensor(out=nmr[:, k, :], in0=mv[:, k, :, 0], scalar=-1.0, in1=rstd[:, k, :],
                                         op0=ALU.mult, op1=ALU.mult).then_inc(self.s_nm, 1)

            def apply(self, act, g, s_put):
                k = g.slot(4)
                if g.follows(2):
                    act.wait_ge(s_put[g.slot(2)], g.back(2).landed(16, 2))
                act.wait_ge(self.s_nm, g.done(1))
                for t in range(U):
                    a = act.activation(done[:, g.slot(2), t, :], val[:, k, t, :], ACT.Identity, bias=nmr[:, k, t:t + 1], scale=rstd[:, k, t:t + 1])
                a.then_inc(self.s_y, 1)

        def node_second(name, table):
            s_x = sems(name + "_z_loaded", 4)
            s_win = sems(name + "_windows_loaded", 4)
            s_dr = sem(name + "_dest_relative")
            s_put = sems(name + "_y_stored", 2)
            s_oh = sem(name + "_onehot_ready")
            s_ag = sem(name + "_sums")
            s_me = sem(name + "_means_ready")
            norm = Norm(name)
            free_finished_phase()
            with nc.Block() as block:
                @block.sync
                def _(sp):
                    regs = [ctx.enter_context(sp.register(name=f"{name}_start{t}")) for t in range(U * UNROLL)]

                    def step(s):
                        if s.real():
                            g = s
                            at = sp.snap(g.base(N)) if not g.static else g.base(N)
                            if g.follows(4):
                                sp.wait_ge(norm.s_v, g.back(4).done(1))
                            sp.dma_start(rows[:, g.slot(4), :, :], node_rows(z_tab, at)).then_inc(s_x[g.slot(4)], 16)
                            if g.follows(4):
                                sp.wait_ge(s_ag, g.back(4).done(1))
                            load_windows(sp, g, table, s_win, regs)
                    run_steps(sp, NODE_GROUPS, 0, step)

                @block.gpsimd
                def _(pool):
                    def step(g):
                        if g.real():
                            relative_dest(pool, g, s_win, s_oh, s_dr)
                    run_steps(pool, NODE_GROUPS, 0, step)

                @block.tensor
                def _(pe):
                    def step(g):
                        if g.real():
                            pe.wait_ge(s_oh, g.done(1))
                            if g.follows(2):
                                pe.wait_ge(s_me, g.back(2).done(1))
                            for t in range(U):
                                mm = pe.matmul(tiles(bank[g.slot(2)])[:, t, :], onehot[:, g.slot(2), t, :], window[:, g.slot(4), t, 0:D],
                                               start=True, stop=True)
                            mm.then_inc(s_ag, 1)
                    run_steps(pe, NODE_GROUPS, 0, step)

                @block.scalar
                def _(act):
                    def step(s):
                        g = s.back(4)
                        if g.real():
                            at = act.snap(g.base(N)) if not g.static else g.base(N)
                            act.wait_ge(norm.s_y, g.done(1))
                            if g.static and g.number == NODE_GROUPS - 1:
                                if g.follows(1):
                                    act.wait_ge(s_put[g.back(1).slot(2)], g.back(1).landed(16, 2))
                            act.dma_start(node_rows(y_tab, at), done[:, g.slot(2), :, :]).then_inc(s_put[g.slot(2)], 16)
                        g = s.back(2)
                        if g.real():
                            norm.deviation(act, g)
                        g = s.back(1)
                        if g.real():
                            if g.follows(2):
                                act.wait_ge(norm.s_v, g.back(2).done(1))
                            act.wait_ge(s_ag, g.done(1))
                            for t in range(U):
                                a = act.activation(agg[:, g.slot(2), t, :], tiles(bank[g.slot(2)])[:, t, :], ACT.Copy,
                                                   scale=inv_count[:, bass.ds(g.number * U + t, 1)])
                            a.then_inc(s_me, 1)
                        g = s.back(3)
                        if g.real():
                            norm.apply(act, g, s_put)
                    run_steps(act, NODE_GROUPS, 4, step)
                    act.wait_ge(s_put[Group(0, NODE_GROUPS - 1, NODE_GROUPS).slot(2)], Group(0, NODE_GROUPS - 1, NODE_GROUPS).landed(16, 2))
                    act.wait_ge(s_put[Group(0, NODE_GROUPS - 2, NODE_GROUPS).slot(2)], Group(0, NODE_GROUPS - 2, NODE_GROUPS).landed(16, 2))

                @block.vector
                def _(dve):
                    def step(s):
                        if s.real():
                            make_onehot(dve, s, s_oh, s_ag, s_dr)
                        g = s.back(2)
                        if g.real():
                            norm.scales(dve, g)
                        g = s.back(1)
                        if g.real():
                            dve.wait_ge(s_x[g.slot(4)], g.landed(16, 4))
                            if g.follows(4):
                                dve.wait_ge(norm.s_y, g.back(4).done(1))
                            dve.wait_ge(s_me, g.done(1))
                            dve.tensor_tensor(val[:, g.slot(4), :, :], agg[:, g.slot(2), :, :], rows[:, g.slot(4), :, :],
                                              ALU.add).then_inc(norm.s_v, 1)
                            norm.moments(dve, g)
                    run_steps(dve, NODE_GROUPS, 2, step)

        def node_third(name, table):
            s_x = sems(name + "_y_loaded", 4)
            s_win = sems(name + "_windows_loaded", 4)
            s_dr = sem(name + "_dest_relative")
            s_put = sems(name + "_out_stored", 2)
            s_oh = sem(name + "_onehot_ready")
            s_ag = sem(name + "_sums")
            s_T = sem(name + "_y_transposed")
            s_xT = sem(name + "_yT_copied")
            s_me = sem(name + "_means_ready")
            s_Tm = sem(name + "_means_transposed")
            s_mT = sem(name + "_meansT_copied")
            s_h = sem(name + "_hidden_products")
            s_hr = sem(name + "_hidden_ready")
            s_o = sem(name + "_out_products")
            s_xb = sem(name + "_y_plus_bias")
            norm = Norm(name)
            free_finished_phase()
            with nc.Block() as block:
                @block.sync
                def _(sp):
                    regs = [ctx.enter_context(sp.register(name=f"{name}_start{t}")) for t in range(U * UNROLL)]

                    def step(s):
                        if s.real():
                            g = s
                            at = sp.snap(g.base(N)) if not g.static else g.base(N)
                            if g.follows(4):
                                sp.wait_ge(s_T, g.back(4).done(1))
                            if g.follows(4):
                                sp.wait_ge(s_xb, g.back(4).done(1))
                            sp.dma_start(rows[:, g.slot(4), :, :], node_rows(y_tab, at)).then_inc(s_x[g.slot(4)], 16)
                            if g.follows(4):
                                sp.wait_ge(s_ag, g.back(4).done(1))
                            load_windows(sp, g, table, s_win, regs)
                        g = s.back(6)
                        if g.real():
                            at = sp.snap(g.base(N)) if not g.static else g.base(N)
                            sp.wait_ge(norm.s_y, g.done(1))
                            if g.static and g.number == NODE_GROUPS - 1:
                                if g.follows(1):
                                    sp.wait_ge(s_put[g.back(1).slot(2)], g.back(1).landed(16, 2))
                            sp.dma_start(node_rows(out, at), done[:, g.slot(2), :, :]).then_inc(s_put[g.slot(2)], 16)
                    run_steps(sp, NODE_GROUPS, 6, step)
                    sp.wait_ge(s_put[Group(0, NODE_GROUPS - 1, NODE_GROUPS).slot(2)], Group(0, NODE_GROUPS - 1, NODE_GROUPS).landed(16, 2))
                    sp.wait_ge(s_put[Group(0, NODE_GROUPS - 2, NODE_GROUPS).slot(2)], Group(0, NODE_GROUPS - 2, NODE_GROUPS).landed(16, 2))

                @block.gpsimd
                def _(pool):
                    def step(s):
                        if s.real():
                            relative_dest(pool, s, s_win, s_oh, s_dr)
                        g = s.back(1)
                        if g.real():
                            if g.follows(4):
                                pool.wait_ge(norm.s_v, g.back(4).done(1))
                            pool.wait_ge(s_x[g.slot(4)], g.landed(16, 4))
                            for t in range(U):
                                p = pool.tensor_tensor(res[:, g.slot(4), t, :], rows[:, g.slot(4), t, :], b2b_bc[:, :], ALU.add)
                            p.then_inc(s_xb, 1)
                    run_steps(pool, NODE_GROUPS, 1, step)

                @block.tensor
                def _(pe):
                    def step(s):
                        if s.real():
                            g = s
                            if g.follows(1):
                                pe.wait_ge(s_xT, g.back(1).done(1))
                            pe.wait_ge(s_x[g.slot(4)], g.landed(16, 4))
                            for t in range(U):
                                mm = pe.transpose(tiles(bank[0])[:, t, :], rows[:, g.slot(4), t, :], ident[:, :])
                            mm.then_inc(s_T, 1)
                        g = s.back(2)
                        if g.real():
                            pe.wait_ge(s_mT, g.done(1))
                            if g.follows(1):
                                pe.wait_ge(s_hr, g.back(1).done(2))
                            for m in range(2):
                                h = bank[4 + m]
                                pe.matmul(h[:, :], w2a[:, 0, m * P:(m + 1) * P], rowsT[:, g.slot(4), :], start=True, stop=False)
                                pe.matmul(h[:, :], w2a[:, 1, m * P:(m + 1) * P], aggT[:, g.slot(2), :], start=False, stop=True).then_inc(s_h, 1)
                        g = s.back(1)
                        if g.real():
                            if g.follows(1):
                                pe.wait_ge(s_mT, g.back(1).done(1))
                            pe.wait_ge(s_me, g.done(1))
                            for t in range(U):
                                mm = pe.transpose(tiles(bank[3])[:, t, :], agg[:, g.slot(2), t, :], ident[:, :])
                            mm.then_inc(s_Tm, 1)
                        g = s.back(3)
                        if g.real():
                            pe.wait_ge(s_hr, g.done(2))
                            if g.follows(1):
                                pe.wait_ge(norm.s_v, g.back(1).done(1))
                            for t in range(U):
                                pe.matmul(tiles(bank[6])[:, t, :], hidT[:, g.slot(2), 0, t * P:(t + 1) * P], w2b[:, 0, :], start=True, stop=False)
                                mm = pe.matmul(tiles(bank[6])[:, t, :], hidT[:, g.slot(2), 1, t * P:(t + 1) * P], w2b[:, 1, :], start=False, stop=True)
                            mm.then_inc(s_o, 1)
                        g = s
                        if g.real():
                            pe.wait_ge(s_oh, g.done(1))
                            if g.follows(1):
                                pe.wait_ge(s_me, g.back(1).done(1))
                            for t in range(U):
                                mm = pe.matmul(tiles(bank[1])[:, t, :], onehot[:, g.slot(2), t, :], window[:, g.slot(4), t, 0:D],
                                               start=True, stop=True)
                            mm.then_inc(s_ag, 1)
                    run_steps(pe, NODE_GROUPS, 3, step)

                @block.scalar
                def _(act):
                    def step(s):
                        if s.real():
                            g = s
                            if g.follows(4):
                                act.wait_ge(s_h, g.back(4).done(2))
                            act.wait_ge(s_T, g.done(1))
                            act.activation(rowsT[:, g.slot(4), :], bank[0][:, :], ACT.Copy).then_inc(s_xT, 1)
                        g = s.back(2)
                        if g.real():
                            if g.follows(2):
                                act.wait_ge(s_o, g.back(2).done(1))
                            for m in range(2):
                                act.wait_ge(s_h, g.number * 2 + (m + 1))
                                act.activation(hidT[:, g.slot(2), m, :], bank[4 + m][:, :], ACT.Relu, bias=c2_col[:, m:m + 1]).then_inc(s_hr, 1)
                        g = s.back(1)
                        if g.real():
                            if g.follows(2):
                                act.wait_ge(s_h, g.back(2).done(2))
                            act.wait_ge(s_Tm, g.done(1))
                            act.activation(aggT[:, g.slot(2), :], bank[3][:, :], ACT.Copy).then_inc(s_mT, 1)
                        g = s.back(3)
                        if g.real():
                            norm.deviation(act, g)
                        g = s.back(4)
                        if g.real():
                            norm.apply(act, g, s_put)
                    run_steps(act, NODE_GROUPS, 4, step)

                @block.vector
                def _(dve):
                    def step(s):
                        if s.real():
                            make_onehot(dve, s, s_oh, s_ag, s_dr)
                        g = s.back(1)
                        if g.real():
                            if g.follows(2):
                                dve.wait_ge(s_Tm, g.back(2).done(1))
                            dve.wait_ge(s_ag, g.done(1))
                            for t in range(U):
                                d = dve.tensor_scalar(agg[:, g.slot(2), t, :], tiles(bank[1])[:, t, :],
                                                      inv_count[:, bass.ds(g.number * U + t, 1)], None, ALU.mult)
                            d.then_inc(s_me, 1)
                        g = s.back(4)
                        if g.real():
                            norm.scales(dve, g)
                        g = s.back(3)
                        if g.real():
                            if g.follows(4):
                                dve.wait_ge(norm.s_y, g.back(4).done(1))
                            dve.wait_ge(s_xb, g.done(1))
                            dve.wait_ge(s_o, g.done(1))
                            dve.tensor_tensor(val[:, g.slot(4), :, :], tiles(bank[6]), res[:, g.slot(4), :, :], ALU.add).then_inc(norm.s_v, 1)
                            norm.moments(dve, g)
                    run_steps(dve, NODE_GROUPS, 4, step)

        edge_conv("conv1", x, w1, messages[0], True)
        node_first("nodes1", messages[0])
        edge_conv("conv2", x1_tab, w2, messages[1], False)
        node_second("nodes2", messages[1])
        edge_mlp("mlp1", y_tab, messages[2])
        node_third("nodes3", messages[2])


_INS = ['x', 'src', 'dst', 'edge_attr_128', 'edge_weight1', 'L0_gnn_W1', 'L0_gnn_root1', 'L0_gnn_b1',
        'L0_gnn_W2', 'L0_gnn_root2', 'L0_gnn_b2', 'L1_gnn_u', 'L1_gnn_W1a', 'L1_gnn_b1a', 'L1_gnn_W1b',
        'L1_gnn_b1b', 'L1_gnn_W2a', 'L1_gnn_b2a', 'L1_gnn_W2b', 'L1_gnn_b2b']


def kernel(**inputs):
    import numpy as _np
    import concourse.bacc as _bacc
    from concourse.bass_utils import run_bass_kernel_spmd as _run

    nc = _bacc.Bacc("TRN2", target_bir_lowering=False, num_devices=1)
    arrays, args = {}, []
    for name in _INS:
        a = _np.ascontiguousarray(inputs[name])
        if name == 'edge_weight1':
            a = a.reshape(-1)
        arrays[f"in_{name}_dram"] = a
        args.append(nc.dram_tensor(f"in_{name}_dram", a.shape, mybir.dt.from_np(a.dtype), kind="ExternalInput").ap())
    out = nc.dram_tensor("out_0_dram", (arrays["in_x_dram"].shape[0], D), F32, kind="ExternalOutput").ap()
    build(nc, *args, out)
    r = _run(nc, [arrays], core_ids=[0])
    return r.results[0]["out_0_dram"]
```

```python
from contextlib import ExitStack

import concourse.bass as bass
from concourse import mybir
from concourse.bass import IndirectOffsetOnAxis

ALU = mybir.AluOpType
ACT = mybir.ActivationFunctionType
F32 = mybir.dt.float32
F32R = mybir.dt.float32r
BF16 = mybir.dt.bfloat16
I32 = mybir.dt.int32
AX = mybir.AxisListType

P = 128
U = 4
GROUP = P * U
D = 128
H = 256
COUNT = D
DEST = D + 1
ROW = D + 2
EPS = 1e-5
UNROLL = 4
LEAD = 8
NO_NODE = -1.0


class Group:

    def __init__(self, i, c, count, over=False):
        self.i, self.c, self.count, self.over = i, c, count, over
        self.static = isinstance(i, int)

    @property
    def number(self):
        return self.i * UNROLL + self.c

    def real(self):
        return not self.over and (not self.static or 0 <= self.number < self.count)

    def back(self, n):
        return Group(self.i, self.c - n, self.count, self.over)

    def at(self, what):
        return what[:, bass.ds(self.number, 1), :].rearrange("p a u -> p (a u)")

    def slot(self, slots):
        return self.c % slots

    def turn(self, slots):
        return self.i * (UNROLL // slots) + self.c // slots

    def follows(self, n):
        return not self.static or self.number >= n

    def done(self, per_group):
        return self.number * per_group + per_group

    def landed(self, per_group, slots):
        return self.turn(slots) * per_group + per_group

    def base(self, rows):
        if self.static:
            return min(GROUP * self.number, rows - GROUP)
        return self.i * (UNROLL * GROUP) + GROUP * self.c


def run_steps(eng, count, depth, step, ahead=0):
    turns = (count - 1 - ahead - LEAD) // UNROLL
    for c in range(LEAD):
        step(Group(0, c, count))
    first = LEAD // UNROLL
    with eng.Fori(first, first + turns) as i:
        for c in range(UNROLL):
            step(Group(i, c, count))
    for c in range(LEAD + turns * UNROLL, count + depth):
        step(Group(0, c, count))


def run_joined_steps(eng, edge_count, node_count, lag, depth, step):
    lead = 2 * LEAD
    both = lead + (edge_count - 1 - 2 - lead) // UNROLL * UNROLL
    alone = -(-(edge_count + lag) // UNROLL) * UNROLL
    last = alone + (node_count - 1 + lag - alone) // UNROLL * UNROLL

    def straight(first, end):
        for c in range(first, end):
            step(Group(0, c, edge_count), Group(0, c - lag, node_count))

    straight(0, lead)
    with eng.Fori(lead // UNROLL, both // UNROLL) as i:
        for c in range(UNROLL):
            step(Group(i, c, edge_count), Group(i, c - lag, node_count))
    straight(both, alone)
    with eng.Fori(alone // UNROLL, last // UNROLL) as i:
        for c in range(UNROLL):
            step(Group(i, c, edge_count, over=True), Group(i, c - lag, node_count))
    straight(last, node_count + lag + depth)


def build(nc, x, src, dst, edge_attr, edge_weight, W1, root1, b1, W2, root2, b2,
          u_glob, W1a, b1a, W1b, b1b, W2a, b2a, W2b, b2b, out):
    N, E = x.shape[0], src.shape[0]
    NODE_GROUPS = -(-N // GROUP)
    EDGE_GROUPS = -(-E // GROUP)
    NT = NODE_GROUPS * U
    FIRST_LAST = N - GROUP
    NEW_IN_LAST = GROUP * (EDGE_GROUPS - 1) - (E - GROUP)
    assert NEW_IN_LAST % U == 0
    SUMMED = E + P
    EDGE_TILES = -(-E // P)
    CHECK_ROWS = max(k for k in range(1, P + 1) if E % k == 0)
    CHECK_COLS = E // CHECK_ROWS

    ctx = ExitStack()
    with ctx:
        def sb(name, shape, dt=F32):
            return ctx.enter_context(nc.sbuf_tensor(name, shape, dt))

        def pb(name, shape, dt=F32):
            return ctx.enter_context(nc.psum_tensor(name, shape, dt))

        held = {"now": [], "before": []}

        def sem(name):
            held["now"].append(nc.alloc_semaphore(name=name))
            return held["now"][-1]

        def free_finished_phase():
            if held["before"]:
                nc.clear_and_free_semaphores(held["before"])
            held["before"], held["now"] = held["now"], []

        def sems(name, n):
            return [sem(f"{name}{k}") for k in range(n)]

        x1_tab = nc.dram_tensor("x1_tab", (N, D), F32).ap()
        z_tab = nc.dram_tensor("z_tab", (N, D), F32).ap()
        y_tab = nc.dram_tensor("y_tab", (N, D), F32).ap()
        messages = [nc.dram_tensor(f"messages{k}", (SUMMED + N, ROW), F32).ap() for k in range(3)]

        ident = sb("ident", [P, P])
        node_iota = sb("node_iota", [P, P])
        starts = sb("starts", [P, NT + 1])
        node_col = sb("node_col", [P, 1])
        here = sb("here", [CHECK_ROWS, CHECK_COLS], I32)
        after = sb("after", [CHECK_ROWS, CHECK_COLS], I32)
        descends = sb("descends", [CHECK_ROWS, CHECK_COLS])
        descents = sb("descents", [CHECK_ROWS, 1])
        disorder = sb("disorder", [1, 1])
        first_row = sb("first_row", [1, NT + 1])
        tile_edges = sb("tile_edges", [1, NT])
        summed_row = sb("summed_row", [1, NT])
        most_edges = sb("most_edges", [1, 1])
        too_many = sb("too_many", [1, 1])
        general = sb("general", [1, 1])
        general_flag = sb("general_flag", [1, 1], I32)
        count_w = sb("count_w", [P, 2], BF16)
        start_row = sb("start_row", [1, -(-NT // (U * UNROLL)) * U * UNROLL], I32)
        inv_count = sb("inv_count", [P, NT])
        pad_rows = sb("pad_rows", [P, ROW])
        eps = sb("eps", [P, 1])
        w1 = sb("w1", [P, 2, D])
        w2 = sb("w2", [P, 2, D])
        r1 = sb("r1", [P, D])
        r2 = sb("r2", [P, D])
        w1a = sb("w1a", [P, 2, H])
        w1b = sb("w1b", [P, 2, D])
        w2a = sb("w2a", [P, 3, H])
        w2b = sb("w2b", [P, 2, D])
        w1a_hi, w1a_lo = sb("w1a_hi", [P, 2, H], F32R), sb("w1a_lo", [P, 2, H], F32R)
        w2a_hi, w2a_lo = sb("w2a_hi", [P, 2, H], F32R), sb("w2a_lo", [P, 2, H], F32R)
        b1_bc = sb("b1_bc", [P, D])
        b2_bc = sb("b2_bc", [P, D])
        b1b_bc = sb("b1b_bc", [P, D])
        b2b_bc = sb("b2b_bc", [P, D])
        b1a_col = sb("b1a_col", [P, 2])
        b2a_col = sb("b2a_col", [P, 2])
        c2_col = sb("c2_col", [P, 2])
        u_col = sb("u_col", [P, 1])

        src_t = sb("src_t", [P, 4, U], I32)
        dst_all = sb("dst_all", [P, EDGE_GROUPS, U], I32)
        u_all = sb("u_all", [P, EDGE_GROUPS, U])
        omu_all = sb("omu_all", [P, EDGE_GROUPS, U])
        below = sb("below", [P, 2, U, NT + 1], BF16)
        rows = sb("rows", [P, 4, U, D])
        rowsT = sb("rowsT", [P, 2, GROUP])
        attr = sb("attr", [P, 2, U, D])
        rowsT_hi, rowsT_lo = sb("rowsT_hi", [P, 4, GROUP], F32R), sb("rowsT_lo", [P, 4, GROUP], F32R)
        sideT_hi, sideT_lo = sb("sideT_hi", [P, 2, GROUP], F32R), sb("sideT_lo", [P, 2, GROUP], F32R)
        hidT = sb("hidT", [P, 2, 2, GROUP])
        part0 = sb("part0", [P, 2, U, D])
        mess = sb("mess", [P, 4, U, ROW])
        window = sb("window", [P, 4, U, ROW])
        dest_rel = sb("dest_rel", [P, 4, U])
        onehot = sb("onehot", [P, 2, U, P])
        agg = sb("agg", [P, 2, U, D])
        aggT = sb("aggT", [P, 2, GROUP])
        cnt = sb("cnt", [P, 2, U])
        res = sb("res", [P, 4, U, D])
        val = sb("val", [P, 4, U, D])
        stats = sb("stats", [P, 4, U, 6])
        mv = sb("mv", [P, 4, U, 2])
        std = sb("std", [P, 4, U])
        rstd = sb("rstd", [P, 4, U])
        nmr = sb("nmr", [P, 4, U])
        done = sb("done", [P, 2, U, D])

        bank = [pb(f"bank{k}", [P, GROUP]) for k in range(8)]

        def tiles(b):
            return b[:, :].rearrange("p (u f) -> p u f", u=U)

        s_w = sem("weights_loaded")
        s_pad = sem("pad_made")
        s_padst = sem("pad_stored")
        s_c0 = sem("const_filled")
        s_c1 = sem("const_ready")
        s_whi = sem("weights_high_ready")
        s_c2 = sem("glob_product")
        s_c2d = sem("glob_added")
        s_ord = sem("order_loaded")
        s_dsc = sem("descents_ready")
        s_dsm = sem("descents_summed")
        s_dis = sem("disorder_ready")
        free_finished_phase()
        with nc.Block() as block:
            @block.sync
            def _(sp):
                for t, w in ((w1[:, :, :], W1.rearrange("k d o -> d k o")), (w2[:, :, :], W2.rearrange("k d o -> d k o")),
                             (r1[:, :], root1), (r2[:, :], root2),
                             (w1a[:, :, :], W1a.rearrange("(k p) n -> p k n", p=P)),
                             (w1b[:, :, :], W1b.rearrange("(k p) n -> p k n", p=P)),
                             (w2a[:, :, :], W2a.rearrange("(k p) n -> p k n", p=P)),
                             (w2b[:, :, :], W2b.rearrange("(k p) n -> p k n", p=P)),
                             (b1_bc[:, :], b1.partition_broadcast(P)), (b2_bc[:, :], b2.partition_broadcast(P)),
                             (b1b_bc[:, :], b1b.partition_broadcast(P)), (b2b_bc[:, :], b2b.partition_broadcast(P))):
                    sp.dma_start(t, w).then_inc(s_w, 16)
                sp.dma_start(b1a_col[:, :], b1a.rearrange("(m p) -> p m", p=P), allow_slow_non_contiguous=True).then_inc(s_w, 16)
                sp.dma_start(b2a_col[:, :], b2a.rearrange("(m p) -> p m", p=P), allow_slow_non_contiguous=True).then_inc(s_w, 16)
                sp.dma_start(u_col[:, :], u_glob[0:1, :].rearrange("a p -> p a"), allow_slow_non_contiguous=True).then_inc(s_w, 16)
                sp.dma_start(here[:, :], dst.rearrange("(p c) -> p c", c=CHECK_COLS)).then_inc(s_ord, 16)
                sp.dma_start(after[0:CHECK_ROWS - 1, :], dst[1:E - CHECK_COLS + 1].rearrange("(p c) -> p c", c=CHECK_COLS)).then_inc(s_ord, 16)
                sp.dma_start(after[CHECK_ROWS - 1:CHECK_ROWS, 0:CHECK_COLS - 1], dst[E - CHECK_COLS + 1:E].rearrange("(p c) -> p c", p=1)).then_inc(s_ord, 16)
                sp.dma_start(after[CHECK_ROWS - 1:CHECK_ROWS, CHECK_COLS - 1:CHECK_COLS], dst[E - 1:E].rearrange("(p c) -> p c", p=1)).then_inc(s_ord, 16)
                sp.wait_ge(s_pad, 2)
                for m in messages:
                    sp.dma_start(m[E:E + P, :], pad_rows[:, :]).then_inc(s_padst, 16)
                sp.wait_ge(s_padst, 16 * len(messages))
                sp.wait_ge(s_w, 16 * 15)
                sp.wait_ge(s_ord, 16 * 4)

            @block.gpsimd
            def _(pool):
                pool.memset(ident[:, :], 0.0).then_inc(s_c0, 1)
                pool.memset(count_w[:, :], 1.0).then_inc(s_c0, 1)
                pool.iota(node_iota[:, :], [[1, P]], base=0, channel_multiplier=0, allow_small_or_imprecise_dtypes=True)
                pool.iota(starts[:, 0:NT - U], [[P, NT - U]], base=0, channel_multiplier=0, allow_small_or_imprecise_dtypes=True)
                pool.iota(starts[:, NT:NT + 1], [[1, 1]], base=(NT - U) * P, channel_multiplier=0, allow_small_or_imprecise_dtypes=True)
                pool.iota(node_col[:, :], [[1, 1]], base=0, channel_multiplier=1, allow_small_or_imprecise_dtypes=True)
                pool.iota(starts[:, NT - U:NT], [[P, U]], base=FIRST_LAST, channel_multiplier=0, allow_small_or_imprecise_dtypes=True)
                pool.wait_ge(s_c0, 2)
                pool.affine_select(out=ident[:, :], in_=ident[:, :], compare_op=ALU.not_equal, fill=1.0,
                                   base=0, pattern=[[-1, P]], channel_multiplier=1)
                pool.affine_select(out=count_w[:, 1:2], in_=count_w[:, 1:2], compare_op=ALU.is_ge, fill=0.0,
                                   base=-(NEW_IN_LAST // U), pattern=[[0, 1]], channel_multiplier=1).then_inc(s_c1, 1)

            @block.tensor
            def _(pe):
                pe.wait_ge(s_w, 16 * 15)
                for m in range(2):
                    mm = pe.matmul(bank[0][:, m:m + 1], w2a[:, 2, m * P:(m + 1) * P], u_col[:, :], start=True, stop=True)
                mm.then_inc(s_c2, 1)
                pe.wait_ge(s_dsc, 2)
                pe.matmul(bank[1][0:1, 0:1], descents[:, :], descents[:, :], start=True, stop=True).then_inc(s_dsm, 1)

            @block.scalar
            def _(act):
                act.wait_ge(s_w, 16 * 15)
                act.activation(w1a_hi[:, :, :], w1a[:, :, :], ACT.Copy)
                act.activation(w2a_hi[:, :, :], w2a[:, 0:2, :], ACT.Copy).then_inc(s_whi, 1)

            @block.vector
            def _(dve):
                dve.memset(pad_rows[:, 0:DEST], 0.0).then_inc(s_pad, 1)
                dve.memset(pad_rows[:, DEST:ROW], NO_NODE).then_inc(s_pad, 1)
                dve.memset(mess[:, :, :, COUNT:COUNT + 1], 1.0)
                dve.memset(eps[:, :], EPS)
                dve.memset(start_row[:, :], 0)
                dve.wait_ge(s_c2, 1)
                dve.tensor_tensor(c2_col[:, :], bank[0][:, 0:2], b2a_col[:, :], ALU.add).then_inc(s_c2d, 1)
                dve.wait_ge(s_whi, 1)
                dve.tensor_tensor(w1a_lo[:, :, :], w1a[:, :, :], w1a_hi[:, :, :], ALU.subtract)
                dve.tensor_tensor(w2a_lo[:, :, :], w2a[:, 0:2, :], w2a_hi[:, :, :], ALU.subtract)
                dve.wait_ge(s_ord, 16 * 4)
                dve.tensor_tensor(descends[:, :], here[:, :], after[:, :], ALU.is_gt).then_inc(s_dsc, 1)
                dve.wait_ge(s_dsc, 1)
                dve.tensor_reduce(descents[:, :], descends[:, :], AX.X, ALU.add).then_inc(s_dsc, 1)
                dve.wait_ge(s_dsm, 1)
                dve.tensor_copy(disorder[:, :], bank[1][0:1, 0:1]).then_inc(s_dis, 1)

        def split_product(pe, h, parts):
            passes = [p for w_hi, w_lo, x_hi, x_lo in parts for p in ((w_hi, x_hi), (w_lo, x_hi), (w_hi, x_lo))]
            for k, (w, x) in enumerate(passes):
                mm = pe.matmul(h, w, x, start=(k == 0), stop=(k == len(passes) - 1))
            return mm

        def edge_values(v, at):
            return v[bass.ds(at, GROUP)].rearrange("(p u) -> p u", u=U)

        class EdgeConv:

            def __init__(self, name, table, w, out_rows, counting):
                self.table, self.w, self.out_rows, self.counting = table, w, out_rows, counting
                self.s_src = sems(name + "_sources_loaded", 4)
                self.s_got = sems(name + "_rows_gathered", 4)
                self.s_go = sem(name + "_gather_released")
                self.s_put = sems(name + "_messages_stored", 4)
                self.s_T = sem(name + "_rows_transposed")
                self.s_xT = sem(name + "_rowsT_copied")
                self.s_mm = sem(name + "_products")
                self.s_t0 = sem(name + "_part0_ready")
                self.s_ms = sem(name + "_messages_ready")
                if counting:
                    self.s_idx = sems(name + "_edges_loaded", 4)
                    self.s_om = sem(name + "_omu_ready")
                    self.s_df = sem(name + "_dest_ready")
                    self.s_bl = sem(name + "_below_ready")
                    self.s_ct = sem(name + "_below_summed")
                    self.s_fr = sem(name + "_first_rows_step")

            def load_sources(self, sp, g):
                if g.real():
                    if g.follows(4):
                        sp.wait_ge(self.s_T, g.back(4).done(1))
                    at = sp.snap(g.base(E)) if not g.static else g.base(E)
                    sp.dma_start(src_t[:, g.slot(4), :], edge_values(src, at)).then_inc(self.s_src[g.slot(4)], 16)

            def first_sources(self, sp):
                for n in range(2):
                    self.load_sources(sp, Group(0, n, EDGE_GROUPS))

            def load_and_store(self, sp, s):
                self.load_sources(sp, s.back(-2))
                if self.counting and s.real():
                    g = s
                    at = sp.snap(g.base(E)) if not g.static else g.base(E)
                    for t, v in ((dst_all, dst), (u_all, edge_weight)):
                        sp.dma_start(g.at(t), edge_values(v, at)).then_inc(self.s_idx[g.slot(4)], 16)
                g = s.back(3)
                if g.real():
                    at = sp.snap(g.base(E)) if not g.static else g.base(E)
                    sp.wait_ge(self.s_ms, g.done(1))
                    if g.static and g.number == EDGE_GROUPS - 1:
                        sp.wait_ge(self.s_put[g.back(1).slot(4)], g.back(1).landed(16, 4))
                    sp.dma_start(self.out_rows[bass.ds(at, GROUP), :].rearrange("(p u) f -> p u f", u=U),
                                 mess[:, g.slot(4), :, :]).then_inc(self.s_put[g.slot(4)], 16)

            def all_stored(self, sp):
                for n in range(EDGE_GROUPS - 4, EDGE_GROUPS):
                    g = Group(0, n, EDGE_GROUPS)
                    sp.wait_ge(self.s_put[g.slot(4)], g.landed(16, 4))

            def gather(self, pool, g, top):
                if g.real():
                    pool.wait_ge(self.s_src[g.slot(4)], g.landed(16, 4))
                    if g.follows(4):
                        pool.wait_ge(self.s_T, g.back(4).done(1))
                    pool.sem_inc(self.s_go, 1)
                    for t in range(U):
                        pool.indirect_dma_start(rows[:, g.slot(4), t, :], None, self.table,
                                                IndirectOffsetOnAxis(ap=src_t[:, g.slot(4), t:t + 1], axis=0),
                                                bounds_check=top, oob_is_err=False).then_inc(self.s_got[g.slot(4)], 16)

            def products(self, pe, s):
                if s.real():
                    g = s
                    if g.follows(1):
                        pe.wait_ge(self.s_xT, g.back(1).done(1))
                    pe.wait_ge(self.s_got[g.slot(4)], g.landed(16 * U, 4))
                    for t in range(U):
                        mm = pe.transpose(tiles(bank[0])[:, t, :], rows[:, g.slot(4), t, :], ident[:, :])
                    mm.then_inc(self.s_T, 1)
                g = s.back(1)
                if g.real():
                    pe.wait_ge(self.s_xT, g.done(1))
                    if g.follows(2):
                        pe.wait_ge(self.s_ms, g.back(2).done(1))
                    for t in range(U):
                        b = bank[1 + 2 * g.slot(2) + t // 2]
                        mm = pe.matmul(b[:, (t % 2) * 2 * D:(t % 2 + 1) * 2 * D], rowsT[:, g.slot(2), t * P:(t + 1) * P],
                                       self.w[:, :, :].rearrange("p k o -> p (k o)"), start=True, stop=True)
                    mm.then_inc(self.s_mm, 1)
                    if self.counting:
                        pe.wait_ge(self.s_bl, g.done(1))
                        last = g.static and g.number == EDGE_GROUPS - 1
                        for t in range(U):
                            mm = pe.matmul(bank[5][0:1, 0:NT + 1], count_w[:, int(last):int(last) + 1], below[:, g.slot(2), t, :],
                                           start=(g.static and g.number == 0 and t == 0), stop=(last and t == U - 1))
                        mm.then_inc(self.s_ct, 1)

            def first_parts(self, act, s):
                if s.real():
                    g = s
                    if g.follows(2):
                        act.wait_ge(self.s_mm, g.back(2).done(1))
                    act.wait_ge(self.s_T, g.done(1))
                    act.activation(rowsT[:, g.slot(2), :], bank[0][:, :], ACT.Copy).then_inc(self.s_xT, 1)
                g = s.back(1)
                if g.real():
                    if self.counting:
                        act.wait_ge(self.s_om, g.done(1))
                    if g.follows(2):
                        act.wait_ge(self.s_ms, g.back(2).done(1))
                    act.wait_ge(self.s_mm, g.done(1))
                    for t in range(U):
                        b = bank[1 + 2 * g.slot(2) + t // 2]
                        a = act.activation(part0[:, g.slot(2), t, :], b[:, (t % 2) * 2 * D:(t % 2) * 2 * D + D], ACT.Copy,
                                           scale=g.at(omu_all)[:, t:t + 1])
                    a.then_inc(self.s_t0, 1)

            def messages(self, dve, s):
                if s.real():
                    g = s
                    if self.counting:
                        dve.wait_ge(self.s_idx[g.slot(4)], g.landed(32, 4))
                        dve.tensor_scalar(g.at(omu_all), g.at(u_all), -1.0, 1.0, ALU.mult, ALU.add).then_inc(self.s_om, 1)
                    if g.follows(4):
                        dve.wait_ge(self.s_put[g.slot(4)], g.back(4).landed(16, 4))
                    d = dve.tensor_copy(mess[:, g.slot(4), :, DEST:ROW].rearrange("p u a -> p (u a)"), g.at(dst_all))
                    if self.counting:
                        d.then_inc(self.s_df, 1)
                        if g.follows(2):
                            dve.wait_ge(self.s_ct, g.back(2).done(1))
                        dve.wait_ge(self.s_df, g.done(1))
                        for t in range(U):
                            d = dve.tensor_scalar(below[:, g.slot(2), t, :], starts[:, :], mess[:, g.slot(4), t, DEST:ROW],
                                                  None, ALU.is_gt)
                        d.then_inc(self.s_bl, 1)
                g = s.back(1)
                if g.real():
                    dve.wait_ge(self.s_t0, g.done(1))
                    for t in range(U):
                        b = bank[1 + 2 * g.slot(2) + t // 2]
                        d = dve.scalar_tensor_tensor(out=mess[:, g.slot(4), t, 0:D], in0=b[:, (t % 2) * 2 * D + D:(t % 2 + 1) * 2 * D],
                                                     scalar=g.at(u_all)[:, t:t + 1], in1=part0[:, g.slot(2), t, :],
                                                     op0=ALU.mult, op1=ALU.add)
                    d.then_inc(self.s_ms, 1)

            def first_rows(self, dve):
                s_fr = self.s_fr
                dve.wait_ge(self.s_ct, EDGE_GROUPS)
                dve.tensor_copy(first_row[:, :], bank[5][0:1, 0:NT + 1]).then_inc(s_fr, 1)
                dve.wait_ge(s_fr, 1)
                dve.tensor_tensor(tile_edges[:, 0:NT - 1], first_row[:, 1:NT], first_row[:, 0:NT - 1], ALU.subtract).then_inc(s_fr, 1)
                dve.wait_ge(s_fr, 2)
                dve.tensor_tensor(tile_edges[:, NT - U - 1:NT - U], first_row[:, NT:NT + 1], first_row[:, NT - U - 1:NT - U],
                                  ALU.subtract).then_inc(s_fr, 1)
                dve.tensor_scalar(tile_edges[:, NT - 1:NT], first_row[:, NT - 1:NT], -1.0, float(E), ALU.mult, ALU.add).then_inc(s_fr, 1)
                dve.wait_ge(s_fr, 4)
                dve.tensor_reduce(most_edges[:, :], tile_edges[:, :], AX.X, ALU.max).then_inc(s_fr, 1)
                dve.wait_ge(s_fr, 5)
                dve.tensor_scalar(too_many[:, :], most_edges[:, :], float(P), None, ALU.is_gt).then_inc(s_fr, 1)
                dve.wait_ge(s_fr, 6)
                dve.scalar_tensor_tensor(out=general[:, :], in0=disorder[:, :], scalar=0.0, in1=too_many[:, :],
                                         op0=ALU.is_gt, op1=ALU.max).then_inc(s_fr, 1)
                dve.scalar_tensor_tensor(out=summed_row[:, :], in0=starts[0:1, 0:NT], scalar=float(SUMMED), in1=first_row[:, 0:NT],
                                         op0=ALU.add, op1=ALU.subtract).then_inc(s_fr, 1)
                dve.wait_ge(s_fr, 8)
                dve.tensor_copy(general_flag[:, :], general[:, :])
                dve.scalar_tensor_tensor(out=start_row[:, 0:NT], in0=summed_row[:, :], scalar=general[:, :], in1=first_row[:, 0:NT],
                                         op0=ALU.mult, op1=ALU.add)

        def edge_phase(e):
            with nc.Block() as block:
                @block.sync
                def _(sp):
                    e.first_sources(sp)
                    run_steps(sp, EDGE_GROUPS, 3, lambda s: e.load_and_store(sp, s), ahead=2)
                    e.all_stored(sp)

                @block.gpsimd
                def _(pool):
                    top = pool.to_reg(N - 1)
                    run_steps(pool, EDGE_GROUPS, 0, lambda s: e.gather(pool, s, top))

                @block.tensor
                def _(pe):
                    run_steps(pe, EDGE_GROUPS, 1, lambda s: e.products(pe, s))

                @block.scalar
                def _(act):
                    run_steps(act, EDGE_GROUPS, 1, lambda s: e.first_parts(act, s))

                @block.vector
                def _(dve):
                    run_steps(dve, EDGE_GROUPS, 1, lambda s: e.messages(dve, s))
                    if e.counting:
                        e.first_rows(dve)

        def edge_mlp(name, table, out_rows):
            s_src = sems(name + "_sources_loaded", 4)
            s_at = sems(name + "_attributes_loaded", 2)
            s_got = sems(name + "_rows_gathered", 4)
            s_go = sem(name + "_gather_released")
            s_put = sems(name + "_messages_stored", 4)
            s_T = sem(name + "_rows_transposed")
            s_aT = sem(name + "_attributes_transposed")
            s_xTc = sem(name + "_rowsT_high_ready")
            s_aTc = sem(name + "_attrT_high_ready")
            s_xL = sem(name + "_rowsT_low_ready")
            s_aL = sem(name + "_attrT_low_ready")
            s_h = sem(name + "_hidden_products")
            s_hr = sem(name + "_hidden_ready")
            s_o = sem(name + "_outputs_products")
            s_df = sem(name + "_dest_ready")
            s_ms = sem(name + "_messages_ready")
            free_finished_phase()
            with nc.Block() as block:
                @block.sync
                def _(sp):
                    def load_sources(g):
                        if g.real():
                            if g.follows(4):
                                sp.wait_ge(s_T, g.back(4).done(1))
                            at = sp.snap(g.base(E)) if not g.static else g.base(E)
                            sp.dma_start(src_t[:, g.slot(4), :], edge_values(src, at)).then_inc(s_src[g.slot(4)], 16)

                    def step(s):
                        load_sources(s.back(-2))
                        if s.real():
                            g = s
                            at = sp.snap(g.base(E)) if not g.static else g.base(E)
                            if g.follows(2):
                                sp.wait_ge(s_aT, g.back(2).done(1))
                            sp.dma_start(attr[:, g.slot(2), :, :],
                                         edge_attr[bass.ds(at, GROUP), :].rearrange("(p u) f -> p u f", u=U)).then_inc(s_at[g.slot(2)], 16)
                        g = s.back(4)
                        if g.real():
                            at = sp.snap(g.base(E)) if not g.static else g.base(E)
                            sp.wait_ge(s_ms, g.done(1))
                            if g.static and g.number == EDGE_GROUPS - 1:
                                if g.follows(1):
                                    sp.wait_ge(s_put[g.back(1).slot(4)], g.back(1).landed(16, 4))
                            sp.dma_start(out_rows[bass.ds(at, GROUP), :].rearrange("(p u) f -> p u f", u=U),
                                         mess[:, g.slot(4), :, :]).then_inc(s_put[g.slot(4)], 16)
                    for n in range(2):
                        load_sources(Group(0, n, EDGE_GROUPS))
                    run_steps(sp, EDGE_GROUPS, 4, step, ahead=2)
                    for n in range(EDGE_GROUPS - 4, EDGE_GROUPS):
                        g = Group(0, n, EDGE_GROUPS)
                        sp.wait_ge(s_put[g.slot(4)], g.landed(16, 4))

                @block.gpsimd
                def _(pool):
                    top = pool.to_reg(N - 1)

                    def step(g):
                        if g.real():
                            pool.wait_ge(s_src[g.slot(4)], g.landed(16, 4))
                            if g.follows(4):
                                pool.wait_ge(s_T, g.back(4).done(1))
                            pool.sem_inc(s_go, 1)
                            for t in range(U):
                                pool.indirect_dma_start(rows[:, g.slot(4), t, :], None, table,
                                                        IndirectOffsetOnAxis(ap=src_t[:, g.slot(4), t:t + 1], axis=0),
                                                        bounds_check=top, oob_is_err=False).then_inc(s_got[g.slot(4)], 16)
                    run_steps(pool, EDGE_GROUPS, 0, step)

                @block.tensor
                def _(pe):
                    def step(s):
                        if s.real():
                            g = s
                            if g.follows(1):
                                pe.wait_ge(s_aL, g.back(1).done(1))
                            pe.wait_ge(s_at[g.slot(2)], g.landed(16, 2))
                            for t in range(U):
                                mm = pe.transpose(tiles(bank[1])[:, t, :], attr[:, g.slot(2), t, :], ident[:, :])
                            mm.then_inc(s_aT, 1)
                            if g.follows(1):
                                pe.wait_ge(s_xL, g.back(1).done(1))
                            pe.wait_ge(s_got[g.slot(4)], g.landed(16 * U, 4))
                            for t in range(U):
                                mm = pe.transpose(tiles(bank[0])[:, t, :], rows[:, g.slot(4), t, :], ident[:, :])
                            mm.then_inc(s_T, 1)
                        g = s.back(1)
                        if g.real():
                            pe.wait_ge(s_aL, g.done(1))
                            pe.wait_ge(s_xL, g.done(1))
                            if g.follows(1):
                                pe.wait_ge(s_hr, g.back(1).done(2))
                            for m in range(2):
                                split_product(pe, bank[2 + m][:, :], [
                                    (w1a_hi[:, 1, m * P:(m + 1) * P], w1a_lo[:, 1, m * P:(m + 1) * P], sideT_hi[:, g.slot(2), :], sideT_lo[:, g.slot(2), :]),
                                    (w1a_hi[:, 0, m * P:(m + 1) * P], w1a_lo[:, 0, m * P:(m + 1) * P], rowsT_hi[:, g.slot(2), :], rowsT_lo[:, g.slot(2), :]),
                                ]).then_inc(s_h, 1)
                        g = s.back(2)
                        if g.real():
                            pe.wait_ge(s_hr, g.done(2))
                            if g.follows(1):
                                pe.wait_ge(s_ms, g.back(1).done(1))
                            for t in range(U):
                                pe.matmul(tiles(bank[4])[:, t, :], hidT[:, g.slot(2), 0, t * P:(t + 1) * P], w1b[:, 0, :], start=True, stop=False)
                                mm = pe.matmul(tiles(bank[4])[:, t, :], hidT[:, g.slot(2), 1, t * P:(t + 1) * P], w1b[:, 1, :], start=False, stop=True)
                            mm.then_inc(s_o, 1)
                    run_steps(pe, EDGE_GROUPS, 2, step)

                @block.scalar
                def _(act):
                    def step(s):
                        if s.real():
                            g = s
                            if g.follows(2):
                                act.wait_ge(s_h, g.back(2).done(2))
                            act.wait_ge(s_aT, g.done(1))
                            act.activation(sideT_hi[:, g.slot(2), :], bank[1][:, :], ACT.Copy).then_inc(s_aTc, 1)
                            act.wait_ge(s_T, g.done(1))
                            act.activation(rowsT_hi[:, g.slot(2), :], bank[0][:, :], ACT.Copy).then_inc(s_xTc, 1)
                        g = s.back(1)
                        if g.real():
                            if g.follows(2):
                                act.wait_ge(s_o, g.back(2).done(1))
                            for m in range(2):
                                act.wait_ge(s_h, g.number * 2 + (m + 1))
                                act.activation(hidT[:, g.slot(2), m, :], bank[2 + m][:, :], ACT.Relu, bias=b1a_col[:, m:m + 1]).then_inc(s_hr, 1)
                    run_steps(act, EDGE_GROUPS, 1, step)

                @block.vector
                def _(dve):
                    def step(s):
                        if s.real():
                            g = s
                            if g.follows(2):
                                dve.wait_ge(s_h, g.back(2).done(2))
                            dve.wait_ge(s_aTc, g.done(1))
                            dve.tensor_tensor(sideT_lo[:, g.slot(2), :], bank[1][:, :], sideT_hi[:, g.slot(2), :], ALU.subtract).then_inc(s_aL, 1)
                            dve.wait_ge(s_xTc, g.done(1))
                            dve.tensor_tensor(rowsT_lo[:, g.slot(2), :], bank[0][:, :], rowsT_hi[:, g.slot(2), :], ALU.subtract).then_inc(s_xL, 1)
                        g = s.back(2)
                        if g.real():
                            if g.follows(4):
                                dve.wait_ge(s_put[g.slot(4)], g.back(4).landed(16, 4))
                            dve.tensor_copy(mess[:, g.slot(4), :, DEST:ROW].rearrange("p u a -> p (u a)"), g.at(dst_all))
                            dve.wait_ge(s_o, g.done(1))
                            for t in range(U):
                                d = dve.tensor_tensor(mess[:, g.slot(4), t, 0:D], tiles(bank[4])[:, t, :], b1b_bc[:, :], ALU.add)
                            d.then_inc(s_ms, 1)
                    run_steps(dve, EDGE_GROUPS, 2, step)

        s_in, s_rl, s_oh_all, s_mm_all, s_sum, s_all, s_out = summing = [
            nc.alloc_semaphore(name="summing_" + what) for what in
            ("messages_loaded", "dest_relative", "onehot_ready", "products", "sums_updated", "sums_complete", "sums_stored")]

        def sum_messages(table):
            edges = window[:, 0, 0, :]
            total = window[:, 1, :, :]

            def node_group(number, first):
                with nc.Block() as block:
                    @block.sync
                    def _(sp):
                        sp.dma_start(edges, table[0:P, :]).then_inc(s_in, 16)
                        with sp.Fori(1, EDGE_TILES) as k:
                            at = sp.snap(k * P)
                            sp.wait_ge(s_mm_all, k)
                            sp.dma_start(edges, table[bass.ds(at, P), :]).then_inc(s_in, 16)
                        sp.wait_ge(s_all, 1)
                        sp.dma_start(table[bass.ds(first + SUMMED, GROUP), :].rearrange("(u p) f -> p u f", p=P), total).then_inc(s_out, 16)
                        sp.wait_ge(s_out, 16)

                    @block.tensor
                    def _(pe):
                        with pe.Fori(0, EDGE_TILES) as k:
                            pe.wait_ge(s_oh_all, k + 1)
                            for u in range(U):
                                mm = pe.matmul(bank[2 + u // 2][:, (u % 2) * 256:(u % 2) * 256 + ROW], onehot[:, 0, u, :], edges,
                                               start=True, stop=True)
                            mm.then_inc(s_mm_all, 1)

                    @block.vector
                    def _(dve):
                        dve.memset(total, 0.0).then_inc(s_sum, 1)
                        with dve.Fori(0, EDGE_TILES) as k:
                            dve.wait_ge(s_in, k * 16 + 16)
                            dve.tensor_tensor(dest_rel[:, 0, :], window[:, 0, 0, DEST:ROW].to_broadcast([P, U]), starts[:, bass.ds(number * U, U)],
                                              ALU.subtract).then_inc(s_rl, 1)
                            dve.wait_ge(s_rl, k + 1)
                            dve.tensor_tensor(onehot[:, 0, :, :], node_iota[:, :].unsqueeze(1).to_broadcast([P, U, P]),
                                              dest_rel[:, 0, :].unsqueeze(2).to_broadcast([P, U, P]), ALU.is_equal).then_inc(s_oh_all, 1)
                            dve.wait_ge(s_mm_all, k + 1)
                            dve.wait_ge(s_sum, k + 1)
                            for b in range(2):
                                d = dve.tensor_tensor(window[:, 1, 2 * b:2 * b + 2, :], window[:, 1, 2 * b:2 * b + 2, :],
                                                      bank[2 + b][:, :].rearrange("p (u f) -> p u f", u=2)[:, :, 0:ROW], ALU.add)
                            d.then_inc(s_sum, 1)
                        dve.wait_ge(s_sum, EDGE_TILES + 1)
                        dve.tensor_tensor(window[:, 1, :, DEST], starts[:, bass.ds(number * U, U)], node_col[:, :].to_broadcast([P, U]),
                                          ALU.add).then_inc(s_all, 1)

                for s in summing:
                    nc.gpsimd.sem_clear(s)
                nc.all_engine_barrier()

            with nc.Fori(0, NODE_GROUPS - 1) as number:
                node_group(number, number * GROUP)
            node_group(NODE_GROUPS - 1, FIRST_LAST)

        regs = [ctx.enter_context(nc.sync.register(name=f"window_start{t}")) for t in range(U * UNROLL)]

        def load_windows(sp, g, table, s_win, regs):
            if g.c % UNROLL == 0:
                sp.load(regs, start_row[0:1, bass.ds(g.number * U, U * UNROLL)])
            for t in range(U):
                at = sp.snap(regs[(g.c % UNROLL) * U + t], min_val=0, max_val=SUMMED + N - P)
                sp.dma_start(window[:, g.slot(4), t, :], table[bass.ds(at, P), :]).then_inc(s_win[g.slot(4)], 16)

        def relative_dest(pool, g, s_win, s_oh, s_dr):
            if g.follows(4):
                pool.wait_ge(s_oh, g.back(4).done(1))
            pool.wait_ge(s_win[g.slot(4)], g.landed(16 * U, 4))
            pool.tensor_tensor(dest_rel[:, g.slot(4), :], window[:, g.slot(4), :, DEST], starts[:, bass.ds(g.number * U, U)],
                               ALU.subtract).then_inc(s_dr, 1)

        def make_onehot(dve, g, s_oh, s_ag, s_dr):
            if g.follows(2):
                dve.wait_ge(s_ag, g.back(2).done(1))
            dve.wait_ge(s_dr, g.done(1))
            dve.tensor_tensor(onehot[:, g.slot(2), :, :], node_iota[:, :].unsqueeze(1).to_broadcast([P, U, P]),
                              dest_rel[:, g.slot(4), :].unsqueeze(2).to_broadcast([P, U, P]), ALU.is_equal).then_inc(s_oh, 1)

        def node_rows(table, at):
            return table[bass.ds(at, GROUP), :].rearrange("(u p) f -> p u f", p=P)

        def node_first(name, table):
            s_x = sems(name + "_x_loaded", 4)
            s_win = sems(name + "_windows_loaded", 4)
            s_dr = sem(name + "_dest_relative")
            s_px1 = sems(name + "_x1_stored", 4)
            s_pz = sems(name + "_z_stored", 2)
            s_T = sem(name + "_x_transposed")
            s_xT = sem(name + "_xT_copied")
            s_oh = sem(name + "_onehot_ready")
            s_ag = sem(name + "_sums")
            s_r1 = sem(name + "_root1_product")
            s_ct = sem(name + "_count_read")
            s_iv = sem(name + "_inverse_ready")
            s_me = sem(name + "_mean_ready")
            s_x1 = sem(name + "_x1_ready")
            s_T1 = sem(name + "_x1_transposed")
            s_x1T = sem(name + "_x1T_copied")
            s_r2 = sem(name + "_root2_product")
            s_xb = sem(name + "_x_plus_bias")
            s_z = sem(name + "_z_ready")
            s_mb = sem(name + "_biased_mean_ready")
            r1_bank = (1, 6)
            x1 = val
            z = done
            x1T = aggT
            free_finished_phase()
            with nc.Block() as block:
                @block.sync
                def _(sp):
                    def step(s):
                        if s.real():
                            g = s
                            at = sp.snap(g.base(N)) if not g.static else g.base(N)
                            if g.follows(4):
                                sp.wait_ge(s_T, g.back(4).done(1))
                            if g.follows(4):
                                sp.wait_ge(s_xb, g.back(4).done(1))
                            sp.dma_start(rows[:, g.slot(4), :, :], node_rows(x, at)).then_inc(s_x[g.slot(4)], 16)
                            if g.follows(4):
                                sp.wait_ge(s_ag, g.back(4).done(1))
                            load_windows(sp, g, table, s_win, regs)
                    run_steps(sp, NODE_GROUPS, 0, step)

                @block.gpsimd
                def _(pool):
                    def step(s):
                        if s.real():
                            relative_dest(pool, s, s_win, s_oh, s_dr)
                        g = s.back(1)
                        if g.real():
                            if g.follows(4):
                                pool.wait_ge(s_z, g.back(4).done(1))
                            pool.wait_ge(s_x[g.slot(4)], g.landed(16, 4))
                            for t in range(U):
                                p = pool.tensor_tensor(res[:, g.slot(4), t, :], rows[:, g.slot(4), t, :], b2_bc[:, :], ALU.add)
                            p.then_inc(s_xb, 1)
                    run_steps(pool, NODE_GROUPS, 1, step)

                @block.tensor
                def _(pe):
                    def step(s):
                        g = s
                        if g.real():
                            if g.follows(1):
                                pe.wait_ge(s_xT, g.back(1).done(1))
                            pe.wait_ge(s_x[g.slot(4)], g.landed(16, 4))
                            for t in range(U):
                                mm = pe.transpose(tiles(bank[0])[:, t, :], rows[:, g.slot(4), t, :], ident[:, :])
                            mm.then_inc(s_T, 1)
                        g = s.back(1)
                        if g.real():
                            pe.wait_ge(s_xT, g.done(1))
                            if g.follows(2):
                                pe.wait_ge(s_x1, g.back(2).done(1))
                            for t in range(U):
                                mm = pe.matmul(tiles(bank[r1_bank[g.slot(2)]])[:, t, :], rowsT[:, g.slot(2), t * P:(t + 1) * P], r1[:, :],
                                               start=True, stop=True)
                            mm.then_inc(s_r1, 1)
                        g = s.back(4)
                        if g.real():
                            pe.wait_ge(s_x1T, g.done(1))
                            if g.follows(1):
                                pe.wait_ge(s_z, g.back(1).done(1))
                            for t in range(U):
                                mm = pe.matmul(tiles(bank[5])[:, t, :], x1T[:, g.slot(2), t * P:(t + 1) * P], r2[:, :], start=True, stop=True)
                            mm.then_inc(s_r2, 1)
                        g = s.back(3)
                        if g.real():
                            if g.follows(1):
                                pe.wait_ge(s_x1T, g.back(1).done(1))
                            pe.wait_ge(s_x1, g.done(1))
                            for t in range(U):
                                mm = pe.transpose(tiles(bank[4])[:, t, :], x1[:, g.slot(4), t, :], ident[:, :])
                            mm.then_inc(s_T1, 1)
                        g = s
                        if g.real():
                            pe.wait_ge(s_oh, g.done(1))
                            if g.follows(1):
                                pe.wait_ge(s_me, g.back(1).done(1))
                            for t in range(U):
                                mm = pe.matmul(bank[2 + t // 2][:, (t % 2) * 256:(t % 2) * 256 + D + 1], onehot[:, g.slot(2), t, :],
                                               window[:, g.slot(4), t, 0:D + 1], start=True, stop=True)
                            mm.then_inc(s_ag, 1)
                    run_steps(pe, NODE_GROUPS, 4, step)

                @block.scalar
                def _(act):
                    def step(s):
                        g = s
                        if g.real():
                            if g.follows(2):
                                act.wait_ge(s_r1, g.back(2).done(1))
                            act.wait_ge(s_T, g.done(1))
                            act.activation(rowsT[:, g.slot(2), :], bank[0][:, :], ACT.Copy).then_inc(s_xT, 1)
                        g = s.back(1)
                        if g.real():
                            if g.follows(2):
                                act.wait_ge(s_mb, g.back(2).done(1))
                            act.wait_ge(s_iv, g.done(1))
                            for t in range(U):
                                a = act.activation(agg[:, g.slot(2), t, :], bank[2 + t // 2][:, (t % 2) * 256:(t % 2) * 256 + D], ACT.Copy,
                                                   scale=inv_count[:, bass.ds(g.number * U + t, 1)])
                            a.then_inc(s_me, 1)
                        g = s.back(3)
                        if g.real():
                            if g.follows(2):
                                act.wait_ge(s_r2, g.back(2).done(1))
                            act.wait_ge(s_T1, g.done(1))
                            act.activation(x1T[:, g.slot(2), :], bank[4][:, :], ACT.Copy).then_inc(s_x1T, 1)
                        g = s.back(3)
                        if g.real():
                            at = act.snap(g.base(N)) if not g.static else g.base(N)
                            act.wait_ge(s_x1, g.done(1))
                            if g.static and g.number == NODE_GROUPS - 1:
                                act.wait_ge(s_px1[g.back(1).slot(4)], g.back(1).landed(16, 4))
                            act.dma_start(node_rows(x1_tab, at), x1[:, g.slot(4), :, :]).then_inc(s_px1[g.slot(4)], 16)
                        g = s.back(5)
                        if g.real():
                            at = act.snap(g.base(N)) if not g.static else g.base(N)
                            act.wait_ge(s_z, g.done(1))
                            if g.static and g.number == NODE_GROUPS - 1:
                                act.wait_ge(s_pz[g.back(1).slot(2)], g.back(1).landed(16, 2))
                            act.dma_start(node_rows(z_tab, at), z[:, g.slot(2), :, :]).then_inc(s_pz[g.slot(2)], 16)
                    run_steps(act, NODE_GROUPS, 5, step)
                    for n in range(NODE_GROUPS - 4, NODE_GROUPS):
                        g = Group(0, n, NODE_GROUPS)
                        act.wait_ge(s_px1[g.slot(4)], g.landed(16, 4))
                    for n in range(NODE_GROUPS - 2, NODE_GROUPS):
                        g = Group(0, n, NODE_GROUPS)
                        act.wait_ge(s_pz[g.slot(2)], g.landed(16, 2))

                @block.vector
                def _(dve):
                    def step(s):
                        g = s.back(1)
                        if g.real():
                            dve.wait_ge(s_ag, g.done(1))
                            for b in range(2):
                                d = dve.tensor_scalar(cnt[:, g.slot(2), 2 * b:2 * b + 2], bank[2 + b][:, D::256], 1.0, None, ALU.max)
                            d.then_inc(s_ct, 1)
                            dve.wait_ge(s_ct, g.done(1))
                            dve.reciprocal(inv_count[:, bass.ds(g.number * U, U)], cnt[:, g.slot(2), :]).then_inc(s_iv, 1)
                        g = s.back(2)
                        if g.real():
                            if g.follows(4):
                                dve.wait_ge(s_px1[g.slot(4)], g.back(4).landed(16, 4))
                                dve.wait_ge(s_T1, g.back(4).done(1))
                            dve.wait_ge(s_r1, g.done(1))
                            dve.wait_ge(s_mb, g.done(1))
                            dve.tensor_tensor(x1[:, g.slot(4), :, :], tiles(bank[r1_bank[g.slot(2)]]), part0[:, g.slot(2), :, :],
                                              ALU.add).then_inc(s_x1, 1)
                        if s.real():
                            make_onehot(dve, s, s_oh, s_ag, s_dr)
                        g = s.back(1)
                        if g.real():
                            if g.follows(2):
                                dve.wait_ge(s_x1, g.back(2).done(1))
                            dve.wait_ge(s_me, g.done(1))
                            dve.tensor_tensor(part0[:, g.slot(2), :, :], agg[:, g.slot(2), :, :],
                                              b1_bc[:, :].unsqueeze(1).to_broadcast([P, U, D]), ALU.add).then_inc(s_mb, 1)
                        g = s.back(4)
                        if g.real():
                            if g.follows(2):
                                dve.wait_ge(s_pz[g.slot(2)], g.back(2).landed(16, 2))
                            dve.wait_ge(s_xb, g.done(1))
                            dve.wait_ge(s_r2, g.done(1))
                            dve.tensor_tensor(z[:, g.slot(2), :, :], tiles(bank[5]), res[:, g.slot(4), :, :], ALU.add).then_inc(s_z, 1)
                    run_steps(dve, NODE_GROUPS, 4, step)

        class Norm:

            def __init__(self, name):
                self.s_v = sem(name + "_value_ready")
                self.s_bs = sem(name + "_stats_ready")
                self.s_go = sem(name + "_aggregation_released")
                self.s_mv = sem(name + "_moments_ready")
                self.s_sd = sem(name + "_deviation_ready")
                self.s_rs = sem(name + "_rstd_ready")
                self.s_nm = sem(name + "_shift_ready")
                self.s_y = sem(name + "_normed")

            def moments(self, dve, g):
                k = g.slot(4)
                dve.wait_ge(self.s_v, g.done(1))
                for t in range(U):
                    d = dve.bn_stats(stats[:, k, t, :], val[:, k, t, :])
                d.then_inc(self.s_bs, 1)
                if g.follows(4):
                    dve.wait_ge(self.s_sd, g.back(4).done(1))
                dve.wait_ge(self.s_bs, g.done(1))
                dve.sem_inc(self.s_go, 1)
                for t in range(U):
                    d = dve.bn_aggr(mv[:, k, t, :], stats[:, k, t, :])
                d.then_inc(self.s_mv, 1)

            def deviation(self, act, g):
                k = g.slot(4)
                act.wait_ge(self.s_mv, g.done(1))
                if g.follows(4):
                    act.wait_ge(self.s_rs, g.back(4).done(1))
                act.activation(std[:, k, :], mv[:, k, :, 1], ACT.Sqrt, bias=eps[:, :]).then_inc(self.s_sd, 1)

            def scales(self, dve, g):
                k = g.slot(4)
                dve.wait_ge(self.s_sd, g.done(1))
                if g.follows(4):
                    dve.wait_ge(self.s_y, g.back(4).done(1))
                dve.reciprocal(rstd[:, k, :], std[:, k, :]).then_inc(self.s_rs, 1)
                dve.wait_ge(self.s_rs, g.done(1))
                dve.scalar_tensor_tensor(out=nmr[:, k, :], in0=mv[:, k, :, 0], scalar=-1.0, in1=rstd[:, k, :],
                                         op0=ALU.mult, op1=ALU.mult).then_inc(self.s_nm, 1)

            def apply(self, act, g, s_put):
                k = g.slot(4)
                if g.follows(2):
                    act.wait_ge(s_put[g.slot(2)], g.back(2).landed(16, 2))
                act.wait_ge(self.s_nm, g.done(1))
                for t in range(U):
                    a = act.activation(done[:, g.slot(2), t, :], val[:, k, t, :], ACT.Identity, bias=nmr[:, k, t:t + 1], scale=rstd[:, k, t:t + 1])
                a.then_inc(self.s_y, 1)

        class NodeSecond:
            sum_bank = (6, 7)

            def __init__(self, name, table):
                self.table = table
                self.s_x = sems(name + "_z_loaded", 4)
                self.s_win = sems(name + "_windows_loaded", 4)
                self.s_dr = sem(name + "_dest_relative")
                self.s_put = sems(name + "_y_stored", 2)
                self.s_oh = sem(name + "_onehot_ready")
                self.s_ag = sem(name + "_sums")
                self.s_me = sem(name + "_means_ready")
                self.norm = Norm(name)

            def load(self, sp, g, regs, edges=None):
                if g.real():
                    if g.follows(4):
                        sp.wait_ge(self.s_ag, g.back(4).done(1))
                    if edges is not None:
                        sp.wait_ge(edges.s_put[g.slot(4)], g.landed(16, 4))
                    load_windows(sp, g, self.table, self.s_win, regs)

            def sums(self, pe, g):
                if g.real():
                    pe.wait_ge(self.s_oh, g.done(1))
                    if g.follows(2):
                        pe.wait_ge(self.s_me, g.back(2).done(1))
                    for t in range(U):
                        mm = pe.matmul(tiles(bank[self.sum_bank[g.slot(2)]])[:, t, :], onehot[:, g.slot(2), t, :], window[:, g.slot(4), t, 0:D],
                                       start=True, stop=True)
                    mm.then_inc(self.s_ag, 1)

            def load_norm_store(self, act, s):
                norm = self.norm
                g = s
                if g.real():
                    at = act.snap(g.base(N)) if not g.static else g.base(N)
                    if g.follows(4):
                        act.wait_ge(norm.s_v, g.back(4).done(1))
                    act.dma_start(res[:, g.slot(4), :, :], node_rows(z_tab, at)).then_inc(self.s_x[g.slot(4)], 16)
                g = s.back(4)
                if g.real():
                    at = act.snap(g.base(N)) if not g.static else g.base(N)
                    act.wait_ge(norm.s_y, g.done(1))
                    if g.static and g.number == NODE_GROUPS - 1:
                        act.wait_ge(self.s_put[g.back(1).slot(2)], g.back(1).landed(16, 2))
                    act.dma_start(node_rows(y_tab, at), done[:, g.slot(2), :, :]).then_inc(self.s_put[g.slot(2)], 16)
                g = s.back(1)
                if g.real():
                    if g.follows(2):
                        act.wait_ge(norm.s_v, g.back(2).done(1))
                    act.wait_ge(self.s_ag, g.done(1))
                    for t in range(U):
                        a = act.activation(agg[:, g.slot(2), t, :], tiles(bank[self.sum_bank[g.slot(2)]])[:, t, :], ACT.Copy,
                                           scale=inv_count[:, bass.ds(g.number * U + t, 1)])
                    a.then_inc(self.s_me, 1)
                g = s.back(2)
                if g.real():
                    norm.deviation(act, g)
                g = s.back(3)
                if g.real():
                    norm.apply(act, g, self.s_put)

            def all_stored(self, act):
                for n in range(NODE_GROUPS - 2, NODE_GROUPS):
                    g = Group(0, n, NODE_GROUPS)
                    act.wait_ge(self.s_put[g.slot(2)], g.landed(16, 2))

            def values(self, dve, s, early=0):
                norm = self.norm
                g = s.back(-early)
                if g.real():
                    make_onehot(dve, g, self.s_oh, self.s_ag, self.s_dr)
                g = s.back(2)
                if g.real():
                    norm.scales(dve, g)
                g = s.back(1)
                if g.real():
                    dve.wait_ge(self.s_x[g.slot(4)], g.landed(16, 4))
                    if g.follows(4):
                        dve.wait_ge(norm.s_y, g.back(4).done(1))
                    dve.wait_ge(self.s_me, g.done(1))
                    dve.tensor_tensor(val[:, g.slot(4), :, :], agg[:, g.slot(2), :, :], res[:, g.slot(4), :, :],
                                      ALU.add).then_inc(norm.s_v, 1)
                    norm.moments(dve, g)

        def node_second_phase(n):
            with nc.Block() as block:
                @block.sync
                def _(sp):
                    run_steps(sp, NODE_GROUPS, 0, lambda s: n.load(sp, s, regs))

                @block.gpsimd
                def _(pool):
                    def step(g):
                        if g.real():
                            relative_dest(pool, g, n.s_win, n.s_oh, n.s_dr)
                    run_steps(pool, NODE_GROUPS, 0, step)

                @block.tensor
                def _(pe):
                    run_steps(pe, NODE_GROUPS, 0, lambda s: n.sums(pe, s))

                @block.scalar
                def _(act):
                    run_steps(act, NODE_GROUPS, 4, lambda s: n.load_norm_store(act, s))
                    n.all_stored(act)

                @block.vector
                def _(dve):
                    run_steps(dve, NODE_GROUPS, 2, lambda s: n.values(dve, s))

        def edges_and_nodes(e, n):
            LOADED, WORKED = 5, 7
            with nc.Block() as block:
                @block.sync
                def _(sp):
                    def step(edges, nodes):
                        e.load_and_store(sp, edges)
                        made = nodes.number < EDGE_GROUPS if nodes.static else edges.real()
                        n.load(sp, nodes, regs, e if made else None)
                    e.first_sources(sp)
                    run_joined_steps(sp, EDGE_GROUPS, NODE_GROUPS, LOADED, 0, step)

                @block.gpsimd
                def _(pool):
                    top = pool.to_reg(N - 1)

                    def step(edges, nodes):
                        e.gather(pool, edges, top)
                        if nodes.back(-1).real():
                            relative_dest(pool, nodes.back(-1), n.s_win, n.s_oh, n.s_dr)
                    run_joined_steps(pool, EDGE_GROUPS, NODE_GROUPS, WORKED, 0, step)

                @block.tensor
                def _(pe):
                    def step(edges, nodes):
                        n.sums(pe, nodes)
                        e.products(pe, edges)
                    run_joined_steps(pe, EDGE_GROUPS, NODE_GROUPS, WORKED, 0, step)

                @block.scalar
                def _(act):
                    def step(edges, nodes):
                        n.load_norm_store(act, nodes)
                        e.first_parts(act, edges)
                    run_joined_steps(act, EDGE_GROUPS, NODE_GROUPS, WORKED, 4, step)
                    n.all_stored(act)

                @block.vector
                def _(dve):
                    def step(edges, nodes):
                        n.values(dve, nodes, early=1)
                        e.messages(dve, edges)
                    run_joined_steps(dve, EDGE_GROUPS, NODE_GROUPS, WORKED, 2, step)

        def node_third(name, table):
            s_x = sems(name + "_y_loaded", 4)
            s_win = sems(name + "_windows_loaded", 4)
            s_dr = sem(name + "_dest_relative")
            s_put = sems(name + "_out_stored", 2)
            s_oh = sem(name + "_onehot_ready")
            s_ag = sem(name + "_sums")
            s_T = sem(name + "_y_transposed")
            s_xT = sem(name + "_yT_high_ready")
            s_xL = sem(name + "_yT_low_ready")
            s_me = sem(name + "_means_ready")
            s_Tm = sem(name + "_means_transposed")
            s_mT = sem(name + "_meansT_high_ready")
            s_mL = sem(name + "_meansT_low_ready")
            s_h = sem(name + "_hidden_products")
            s_hr = sem(name + "_hidden_ready")
            s_o = sem(name + "_out_products")
            s_xb = sem(name + "_y_plus_bias")
            norm = Norm(name)
            free_finished_phase()
            with nc.Block() as block:
                @block.sync
                def _(sp):
                    def step(s):
                        if s.real():
                            g = s
                            at = sp.snap(g.base(N)) if not g.static else g.base(N)
                            if g.follows(4):
                                sp.wait_ge(s_T, g.back(4).done(1))
                            if g.follows(4):
                                sp.wait_ge(s_xb, g.back(4).done(1))
                            sp.dma_start(rows[:, g.slot(4), :, :], node_rows(y_tab, at)).then_inc(s_x[g.slot(4)], 16)
                            if g.follows(4):
                                sp.wait_ge(s_ag, g.back(4).done(1))
                            load_windows(sp, g, table, s_win, regs)
                        g = s.back(6)
                        if g.real():
                            at = sp.snap(g.base(N)) if not g.static else g.base(N)
                            sp.wait_ge(norm.s_y, g.done(1))
                            if g.static and g.number == NODE_GROUPS - 1:
                                if g.follows(1):
                                    sp.wait_ge(s_put[g.back(1).slot(2)], g.back(1).landed(16, 2))
                            sp.dma_start(node_rows(out, at), done[:, g.slot(2), :, :]).then_inc(s_put[g.slot(2)], 16)
                    run_steps(sp, NODE_GROUPS, 6, step)
                    sp.wait_ge(s_put[Group(0, NODE_GROUPS - 1, NODE_GROUPS).slot(2)], Group(0, NODE_GROUPS - 1, NODE_GROUPS).landed(16, 2))
                    sp.wait_ge(s_put[Group(0, NODE_GROUPS - 2, NODE_GROUPS).slot(2)], Group(0, NODE_GROUPS - 2, NODE_GROUPS).landed(16, 2))

                @block.gpsimd
                def _(pool):
                    def step(s):
                        if s.real():
                            relative_dest(pool, s, s_win, s_oh, s_dr)
                        g = s.back(1)
                        if g.real():
                            if g.follows(4):
                                pool.wait_ge(norm.s_v, g.back(4).done(1))
                            pool.wait_ge(s_x[g.slot(4)], g.landed(16, 4))
                            for t in range(U):
                                p = pool.tensor_tensor(res[:, g.slot(4), t, :], rows[:, g.slot(4), t, :], b2b_bc[:, :], ALU.add)
                            p.then_inc(s_xb, 1)
                    run_steps(pool, NODE_GROUPS, 1, step)

                @block.tensor
                def _(pe):
                    def step(s):
                        if s.real():
                            g = s
                            if g.follows(1):
                                pe.wait_ge(s_xL, g.back(1).done(1))
                            pe.wait_ge(s_x[g.slot(4)], g.landed(16, 4))
                            for t in range(U):
                                mm = pe.transpose(tiles(bank[0])[:, t, :], rows[:, g.slot(4), t, :], ident[:, :])
                            mm.then_inc(s_T, 1)
                        g = s.back(2)
                        if g.real():
                            pe.wait_ge(s_xL, g.done(1))
                            pe.wait_ge(s_mL, g.done(1))
                            if g.follows(1):
                                pe.wait_ge(s_hr, g.back(1).done(2))
                            for m in range(2):
                                split_product(pe, bank[4 + m][:, :], [
                                    (w2a_hi[:, 0, m * P:(m + 1) * P], w2a_lo[:, 0, m * P:(m + 1) * P], rowsT_hi[:, g.slot(4), :], rowsT_lo[:, g.slot(4), :]),
                                    (w2a_hi[:, 1, m * P:(m + 1) * P], w2a_lo[:, 1, m * P:(m + 1) * P], sideT_hi[:, g.slot(2), :], sideT_lo[:, g.slot(2), :]),
                                ]).then_inc(s_h, 1)
                        g = s.back(1)
                        if g.real():
                            if g.follows(1):
                                pe.wait_ge(s_mL, g.back(1).done(1))
                            pe.wait_ge(s_me, g.done(1))
                            for t in range(U):
                                mm = pe.transpose(tiles(bank[3])[:, t, :], agg[:, g.slot(2), t, :], ident[:, :])
                            mm.then_inc(s_Tm, 1)
                        g = s.back(3)
                        if g.real():
                            pe.wait_ge(s_hr, g.done(2))
                            if g.follows(1):
                                pe.wait_ge(norm.s_v, g.back(1).done(1))
                            for t in range(U):
                                pe.matmul(tiles(bank[6])[:, t, :], hidT[:, g.slot(2), 0, t * P:(t + 1) * P], w2b[:, 0, :], start=True, stop=False)
                                mm = pe.matmul(tiles(bank[6])[:, t, :], hidT[:, g.slot(2), 1, t * P:(t + 1) * P], w2b[:, 1, :], start=False, stop=True)
                            mm.then_inc(s_o, 1)
                        g = s
                        if g.real():
                            pe.wait_ge(s_oh, g.done(1))
                            if g.follows(1):
                                pe.wait_ge(s_me, g.back(1).done(1))
                            for t in range(U):
                                mm = pe.matmul(tiles(bank[1])[:, t, :], onehot[:, g.slot(2), t, :], window[:, g.slot(4), t, 0:D],
                                               start=True, stop=True)
                            mm.then_inc(s_ag, 1)
                    run_steps(pe, NODE_GROUPS, 3, step)

                @block.scalar
                def _(act):
                    def step(s):
                        g = s.back(4)
                        if g.real():
                            norm.deviation(act, g)
                        if s.real():
                            g = s
                            if g.follows(4):
                                act.wait_ge(s_h, g.back(4).done(2))
                            act.wait_ge(s_T, g.done(1))
                            act.activation(rowsT_hi[:, g.slot(4), :], bank[0][:, :], ACT.Copy).then_inc(s_xT, 1)
                        g = s.back(2)
                        if g.real():
                            if g.follows(2):
                                act.wait_ge(s_o, g.back(2).done(1))
                            for m in range(2):
                                act.wait_ge(s_h, g.number * 2 + (m + 1))
                                act.activation(hidT[:, g.slot(2), m, :], bank[4 + m][:, :], ACT.Relu, bias=c2_col[:, m:m + 1]).then_inc(s_hr, 1)
                        g = s.back(1)
                        if g.real():
                            if g.follows(2):
                                act.wait_ge(s_h, g.back(2).done(2))
                            act.wait_ge(s_Tm, g.done(1))
                            act.activation(sideT_hi[:, g.slot(2), :], bank[3][:, :], ACT.Copy).then_inc(s_mT, 1)
                        g = s.back(4)
                        if g.real():
                            norm.apply(act, g, s_put)
                    run_steps(act, NODE_GROUPS, 4, step)

                @block.vector
                def _(dve):
                    def step(s):
                        g = s.back(1)
                        if g.real():
                            if g.follows(2):
                                dve.wait_ge(s_Tm, g.back(2).done(1))
                            dve.wait_ge(s_ag, g.done(1))
                            for t in range(U):
                                d = dve.tensor_scalar(agg[:, g.slot(2), t, :], tiles(bank[1])[:, t, :],
                                                      inv_count[:, bass.ds(g.number * U + t, 1)], None, ALU.mult)
                            d.then_inc(s_me, 1)
                        if s.real():
                            make_onehot(dve, s, s_oh, s_ag, s_dr)
                        g = s
                        if g.real():
                            if g.follows(4):
                                dve.wait_ge(s_h, g.back(4).done(2))
                            dve.wait_ge(s_xT, g.done(1))
                            dve.tensor_tensor(rowsT_lo[:, g.slot(4), :], bank[0][:, :], rowsT_hi[:, g.slot(4), :], ALU.subtract).then_inc(s_xL, 1)
                        g = s.back(4)
                        if g.real():
                            norm.scales(dve, g)
                        g = s.back(1)
                        if g.real():
                            if g.follows(2):
                                dve.wait_ge(s_h, g.back(2).done(2))
                            dve.wait_ge(s_mT, g.done(1))
                            dve.tensor_tensor(sideT_lo[:, g.slot(2), :], bank[3][:, :], sideT_hi[:, g.slot(2), :], ALU.subtract).then_inc(s_mL, 1)
                        g = s.back(3)
                        if g.real():
                            if g.follows(4):
                                dve.wait_ge(norm.s_y, g.back(4).done(1))
                            dve.wait_ge(s_xb, g.done(1))
                            dve.wait_ge(s_o, g.done(1))
                            dve.tensor_tensor(val[:, g.slot(4), :, :], tiles(bank[6]), res[:, g.slot(4), :, :], ALU.add).then_inc(norm.s_v, 1)
                            norm.moments(dve, g)
                    run_steps(dve, NODE_GROUPS, 4, step)

        conv1 = EdgeConv("conv1", x, w1, messages[0], True)
        free_finished_phase()
        edge_phase(conv1)
        flag = nc.values_load(general_flag[0:1, 0:1], min_val=0, max_val=1)
        with nc.If(flag > 0):
            sum_messages(messages[0])
        node_first("nodes1", messages[0])

        conv2 = EdgeConv("conv2", x1_tab, w2, messages[1], False)
        nodes2 = NodeSecond("nodes2", messages[1])
        free_finished_phase()
        with nc.If(flag > 0):
            edge_phase(conv2)
            sum_messages(messages[1])
            node_second_phase(nodes2)
        with nc.Else():
            edges_and_nodes(conv2, nodes2)

        edge_mlp("mlp1", y_tab, messages[2])
        with nc.If(flag > 0):
            sum_messages(messages[2])
        node_third("nodes3", messages[2])


_INS = ['x', 'src', 'dst', 'edge_attr_128', 'edge_weight1', 'L0_gnn_W1', 'L0_gnn_root1', 'L0_gnn_b1',
        'L0_gnn_W2', 'L0_gnn_root2', 'L0_gnn_b2', 'L1_gnn_u', 'L1_gnn_W1a', 'L1_gnn_b1a', 'L1_gnn_W1b',
        'L1_gnn_b1b', 'L1_gnn_W2a', 'L1_gnn_b2a', 'L1_gnn_W2b', 'L1_gnn_b2b']


def kernel(**inputs):
    import numpy as _np
    import concourse.bacc as _bacc
    from concourse.bass_utils import run_bass_kernel_spmd as _run

    nc = _bacc.Bacc("TRN2", target_bir_lowering=False, num_devices=1)
    arrays, args = {}, []
    for name in _INS:
        a = _np.ascontiguousarray(inputs[name])
        if name == 'edge_weight1':
            a = a.reshape(-1)
        arrays[f"in_{name}_dram"] = a
        args.append(nc.dram_tensor(f"in_{name}_dram", a.shape, mybir.dt.from_np(a.dtype), kind="ExternalInput").ap())
    out = nc.dram_tensor("out_0_dram", (arrays["in_x_dram"].shape[0], D), F32, kind="ExternalOutput").ap()
    build(nc, *args, out)
    r = _run(nc, [arrays], core_ids=[0])
    return r.results[0]["out_0_dram"]
```
